# Optimizing a Trainium2 kernel written in Bass

```python
import numpy as np
import jax
import jax.numpy as jnp

def _softmax(x, axis=-1):
    return jax.nn.softmax(x, axis=axis)

def _gelu(x):
    return jax.nn.gelu(x, approximate=True)

def _silu(x):
    return jax.nn.silu(x)

def _sigmoid(x):
    return jax.nn.sigmoid(x)

def _layernorm(x, axis=-1, eps=1e-05):
    m = jnp.mean(x, axis=axis, keepdims=True)
    v = jnp.var(x, axis=axis, keepdims=True)
    return (x - m) / jnp.sqrt(v + eps)

def _scatter_add(tgt, idx, src, axis=0):
    return tgt.at[idx].add(src)

def _segment_sum(src, seg, n):
    return jax.ops.segment_sum(src, seg, n)
kernel_name = 'mk_flamingo_gated_d1_seqx_r4_0554d2'

def setup_inputs(seed: int=0):
    np.random.seed(seed)
    _w = jnp.asarray

    def _rec_inputs():
        import jax
        import jax.numpy as jnp
        _rk = jax.random.key(seed)
        x = 7.22e-05 + 1 * jax.random.normal(jax.random.fold_in(_rk, 1), (8, 256, 256), jnp.float32)
        _lenS = 256 - jax.random.randint(jax.random.fold_in(_rk, 7), (8,), 0, max(1, 256 // 4) + 1, jnp.int32)
        _lenS2 = 120 - jax.random.randint(jax.random.fold_in(_rk, 8), (8,), 0, max(1, 120 // 4) + 1, jnp.int32)
        _ctx_768P = jax.random.normal(jax.random.fold_in(_rk, 11), (8, 16, 192), jnp.float32)
        _ctx_768c = jax.random.dirichlet(jax.random.fold_in(_rk, 511), 0.3 * jnp.ones((16,), jnp.float32), (8, 120))
        _ctx_768t = jnp.einsum('bsk,bkd->bsd', _ctx_768c, _ctx_768P)
        _ctx_768t = _ctx_768t * jax.lax.rsqrt(jnp.mean(jnp.square(_ctx_768t)) + 1e-12) * 0.953939
        ctx_768 = 2.09791e-05 + 1.00001 * (_ctx_768t + 0.3 * jax.random.normal(jax.random.fold_in(_rk, 611), (8, 120, 192), jnp.float32))
        _g = jax.random.normal(jax.random.fold_in(_rk, 9001), (2, 1), jnp.float32)
        _g = jnp.sign(_g) * jnp.maximum(jnp.abs(_g), 1.0) + (_g == 0) * 1.0
        g_xattn = _g[0]
        g_ffn = _g[1]
        return (x, ctx_768, g_xattn, g_ffn)
    x, ctx_768, g_xattn, g_ffn = _rec_inputs()

    def _L0_xattn_setup():
        import jax, jax.numpy as jnp
        import numpy as np
        HEADS = 8
        DIM_HEAD = 64
        SCALE = DIM_HEAD ** (-0.5)
        key = jax.random.key(seed)
        ks = jax.random.split(key, 7)
        b, n, m = (4, 512, 256)
        qd, cd, inner = (256, 192, HEADS * DIM_HEAD)
        s = lambda fan_in: 1.0 / np.sqrt(fan_in)
        return {'x': jax.random.normal(ks[0], (b, n, qd), jnp.float32), 'context': jax.random.normal(ks[1], (b, m, cd), jnp.float32), 'Wq': jax.random.normal(ks[2], (qd, inner), jnp.float32) * s(qd), 'Wk': jax.random.normal(ks[3], (cd, inner), jnp.float32) * s(cd), 'Wv': jax.random.normal(ks[4], (cd, inner), jnp.float32) * s(cd), 'Wout': jax.random.normal(ks[5], (inner, qd), jnp.float32) * s(inner), 'bout': jax.random.normal(ks[6], (qd,), jnp.float32) * 0.01}
    _L0_xattn_all = _L0_xattn_setup()
    _L0_xattn_in = {k: v for k, v in _L0_xattn_all.items() if k in ('Wq', 'Wk', 'Wv', 'Wout', 'bout')}
    del _L0_xattn_all

    def _L0_ffn_setup():
        import jax, jax.numpy as jnp
        import numpy as np
        B, S, H = (4, 512, 256)
        D = 512
        E = 8
        K = 2
        key = jax.random.key(seed)
        ks = jax.random.split(key, 8)
        w = lambda k, shape: jax.random.normal(k, shape, jnp.float32) * 0.02
        return {'hidden_states': jax.random.normal(ks[0], (B, S, H), jnp.float32), 'gate_w': w(ks[1], (H, E)), 'w_gate': w(ks[2], (E, H, D)), 'w_up': w(ks[3], (E, H, D)), 'w_down': w(ks[4], (E, D, H)), 'ws_gate': w(ks[5], (H, D)), 'ws_up': w(ks[6], (H, D)), 'ws_down': w(ks[7], (D, H))}
    _L0_ffn_all = _L0_ffn_setup()
    _L0_ffn_in = {k: v for k, v in _L0_ffn_all.items() if k in ('gate_w', 'w_gate', 'w_up', 'w_down', 'ws_gate', 'ws_up', 'ws_down')}
    del _L0_ffn_all
    return {'x': x, 'ctx_768': ctx_768, 'g_xattn': g_xattn, 'g_ffn': g_ffn, 'L0_xattn_Wq': _L0_xattn_in['Wq'], 'L0_xattn_Wk': _L0_xattn_in['Wk'], 'L0_xattn_Wv': _L0_xattn_in['Wv'], 'L0_xattn_Wout': _L0_xattn_in['Wout'], 'L0_xattn_bout': _L0_xattn_in['bout'], 'L0_ffn_gate_w': _L0_ffn_in['gate_w'], 'L0_ffn_w_gate': _L0_ffn_in['w_gate'], 'L0_ffn_w_up': _L0_ffn_in['w_up'], 'L0_ffn_w_down': _L0_ffn_in['w_down'], 'L0_ffn_ws_gate': _L0_ffn_in['ws_gate'], 'L0_ffn_ws_up': _L0_ffn_in['ws_up'], 'L0_ffn_ws_down': _L0_ffn_in['ws_down']}

def reference(x, ctx_768, g_xattn, g_ffn, L0_xattn_Wq, L0_xattn_Wk, L0_xattn_Wv, L0_xattn_Wout, L0_xattn_bout, L0_ffn_gate_w, L0_ffn_w_gate, L0_ffn_w_up, L0_ffn_w_down, L0_ffn_ws_gate, L0_ffn_ws_up, L0_ffn_ws_down):
    import jax
    import jax.numpy as jnp

    def _L0_xattn_ref(x, context, Wq, Wk, Wv, Wout, bout):
        import jax, jax.numpy as jnp
        import numpy as np
        HEADS = 8
        DIM_HEAD = 64
        SCALE = DIM_HEAD ** (-0.5)
        b, n, _ = x.shape
        m = context.shape[1]
        q = (x @ Wq).reshape(b, n, HEADS, DIM_HEAD)
        k = (context @ Wk).reshape(b, m, HEADS, DIM_HEAD)
        v = (context @ Wv).reshape(b, m, HEADS, DIM_HEAD)
        sim = jnp.einsum('bihd,bjhd->bhij', q, k) * SCALE
        attn = jax.nn.softmax(sim, axis=-1)
        out = jnp.einsum('bhij,bjhd->bihd', attn, v).reshape(b, n, HEADS * DIM_HEAD)
        return out @ Wout + bout

    def _L0_ffn_ref(hidden_states, gate_w, w_gate, w_up, w_down, ws_gate, ws_up, ws_down):
        import jax, jax.numpy as jnp
        import numpy as np
        B, S, H = (4, 512, 256)
        D = 512
        E = 8
        K = 2
        b, s, h = hidden_states.shape
        x = hidden_states.reshape(-1, h)
        scores = jax.nn.softmax(x @ gate_w, axis=-1)
        topk_w, topk_idx = jax.lax.top_k(scores, K)
        topk_w = topk_w / (jnp.sum(topk_w, axis=-1, keepdims=True) + 1e-20)
        onehot = jax.nn.one_hot(topk_idx, E, dtype=x.dtype)
        w_per_expert = jnp.einsum('nke,nk->ne', onehot, topk_w)
        y = jnp.zeros_like(x)
        for e in range(E):
            hid = jax.nn.silu(x @ w_gate[e]) * (x @ w_up[e])
            y = y + w_per_expert[:, e:e + 1] * (hid @ w_down[e])
        shared = jax.nn.silu(x @ ws_gate) * (x @ ws_up) @ ws_down
        return (y + shared).reshape(b, s, h)
    x = x + jnp.tanh(g_xattn[0]) * _L0_xattn_ref(_layernorm(x, axis=-1), ctx_768, L0_xattn_Wq, L0_xattn_Wk, L0_xattn_Wv, L0_xattn_Wout, L0_xattn_bout)
    x = x + jnp.tanh(g_ffn[0]) * _L0_ffn_ref(_layernorm(x, axis=-1), L0_ffn_gate_w, L0_ffn_w_gate, L0_ffn_w_up, L0_ffn_w_down, L0_ffn_ws_gate, L0_ffn_ws_up, L0_ffn_ws_down)
    return x

_drawn_inputs = setup_inputs


def setup_inputs(seed=0):
    import zlib

    import numpy as np

    out = dict(_drawn_inputs(seed))
    spreads = {}
    factors = {'L0_xattn_bout': 7.648,
     'L0_ffn_gate_w': 4.405,
     'L0_ffn_w_gate': 3.856,
     'L0_ffn_w_up': 3.81,
     'L0_ffn_w_down': 3.815,
     'L0_ffn_ws_gate': 2.75,
     'L0_ffn_ws_up': 2.699,
     'L0_ffn_ws_down': 2.715}
    for name, (base, spread) in spreads.items():
        noise = np.random.default_rng([zlib.crc32(name.encode()), seed]).standard_normal(out[name].shape)
        drawn = base * np.exp(spread * noise) if base else spread * noise
        out[name] = jnp.asarray(drawn.astype(out[name].dtype))
    for name, factor in factors.items():
        out[name] = (out[name] * factor).astype(out[name].dtype)
    return out
```

```python
from contextlib import ExitStack

import concourse.bass as bass
from concourse import mybir

F32 = mybir.dt.float32
F32R = mybir.dt.float32r
U32 = mybir.dt.uint32
I32 = mybir.dt.int32
ALU = mybir.AluOpType
ACT = mybir.ActivationFunctionType
AX = mybir.AxisListType

P = 128
HEADS = 8
DH = 64
PAIRS = HEADS // 2
EPS = 1e-5

HI, LO = 0, 1
PASSES = ((HI, HI), (HI, LO), (LO, HI))


def build(nc, x, ctx_in, g_xattn, g_ffn, wq, wk, wv, wo, bout, gate_w, w_gate, w_up, w_down,
          ws_gate, ws_up, ws_down, out):
    B, S, H = x.shape
    _, M, C = ctx_in.shape
    INNER = HEADS * DH
    KT = H // P
    CT = 2
    CP = C // CT
    QT = S // P
    MT = INNER // P
    T = B * QT
    SCALE = DH ** -0.5

    N = B * S
    E, _, D = w_gate.shape
    KD = D // P
    TOP = 2
    R = QT * P
    SHARED = N // R
    ROUTED = N * TOP // R + E
    TILES = SHARED + ROUTED
    RW = H + 2
    IDC, WC = H, H + 1
    GW = 2 * KT * D
    RAW = GW + KD * H
    EARLY = 6

    xg = nc.dram_tensor("xg", (N + ROUTED * R, RW), F32, kind="Internal").ap()

    es = ExitStack()
    early = ExitStack()
    with es:
        def sb(name, shape, dt=F32):
            return es.enter_context(nc.sbuf_tensor(name, shape, dt))

        def sb_attn(name, shape, dt=F32):
            return early.enter_context(nc.sbuf_tensor(name, shape, dt))

        def sem(name):
            return es.enter_context(nc.semaphore(name))

        psum = es.enter_context(nc.psum_tensor("psum", [P, 8, 512], F32))
        SCORES = [psum[:, 0:2], psum[:, 2:4]]
        BC0, BC1, BD, BE = psum[:, 4], psum[:, 5], psum[:, 6], psum[:, 7]

        GATE, UP = [psum[:, 0], psum[:, 2]], [psum[:, 1], psum[:, 3]]
        YB, TXB = [psum[:, 4, 0:H], psum[:, 5, 0:H]], psum[:, 6]

        ident = sb("ident", [P, P])
        half = sb("half", [P, QT])
        gx = sb("gx", [P, 2])
        tg = sb("tg", [P, 2])
        xr = [sb(f"xr{k}", [P, T, RW]) for k in range(TOP)]
        xn2 = sb("xn2", [P, QT, H])
        x2T = sb("x2T", [P, 2, KT, S], F32R)
        gw_raw = sb("gw_raw", [P, KT, E])
        gw_s = sb("gw_s", [P, 2, KT, E], F32R)
        stats2 = sb("stats2", [P, QT, 6])
        mv2 = sb("mv2", [P, QT, 2])
        vare2 = sb("vare2", [P, QT])
        rstd2 = sb("rstd2", [P, QT])
        logit = sb("logit", [P, T, E])
        ones = sb("ones", [P, P])
        before = sb("before", [P, P])
        less = sb("less", [P, E, E])
        more = sb("more", [P, E, E])
        count_i = sb("count_i", [P, ROUTED], I32)
        count = sb("count", [P, ROUTED])
        count_r = sb("count_r", [P, E])
        etab = sb("etab", [1, TILES], I32)
        pos = sb("pos", [P, TOP, T], U32)
        pad = sb("pad", [P, QT, RW])

        rows = sb_attn("rows", [P, T, H])
        crow = sb_attn("crow", [M, B, C])
        cbuf = sb_attn("cbuf", [M, C])
        wstage = sb_attn("wstage", [P, 2, 1024])
        wq_s = sb_attn("wq_s", [P, 2, KT, INNER], F32R)
        wk_s = sb_attn("wk_s", [CP, 2, CT, INNER], F32R)
        wv_s = sb_attn("wv_s", [CP, 2, CT, INNER], F32R)
        wo_s = sb_attn("wo_s", [P, 2, MT, H], F32R)
        bias = sb_attn("bias", [P, H])

        stats = sb_attn("stats", [P, QT, 6])
        mv = sb_attn("mv", [P, QT, 2])
        vare = sb_attn("vare", [P, QT])
        rstd = sb_attn("rstd", [P, QT])
        xn = sb_attn("xn", [P, QT, H])
        xT = sb_attn("xT", [P, 2, KT, S], F32R)
        cT = sb_attn("cT", [CP, 2, CT, M], F32R)
        qT = sb_attn("qT", [P, 2, MT, S], F32R)
        kT = sb_attn("kT", [P, 2, MT, M], F32R)
        vz = sb_attn("vz", [M, 2, HEADS, P], F32R)
        prob = sb_attn("prob", [P, QT, 2, PAIRS, M])
        mx = sb_attn("mx", [P, QT, 2, PAIRS])
        den = sb_attn("den", [P, QT, 2, PAIRS])
        rden = sb_attn("rden", [P, QT, 2, PAIRS])
        pT = sb_attn("pT", [M, 2, HEADS, S], F32R)
        oT = sb_attn("oT", [P, 2, PAIRS, S], F32R)
        early.close()

        sb_attn("gap", [P, T, H])
        small = [sb_attn(f"small{n}", [P, T]) for n in range(6)]
        score = sb_attn("score", [P, T, E])
        rank = sb_attn("rank", [P, T, E])
        sel = [sb_attn(f"sel{k}", [P, T, E]) for k in range(TOP)]
        mask = sb_attn("mask", [P, T, E])
        inside = sb_attn("inside", [P, T, E])
        total = sb_attn("total", [P, T, E])
        cum = [sb_attn(f"cum{n}", [P, T, E]) for n in range(2)]
        slot = sb_attn("slot", [P, T, E])
        picked = sb_attn("picked", [P, T, E])
        square = sb_attn("square", [P, E, E])
        square2 = sb_attn("square2", [P, E, E])
        tiles_e = sb_attn("tiles_e", [P, E])
        base_e = sb_attn("base_e", [P, E])
        owner = sb_attn("owner", [1, ROUTED, E])
        owner_f = sb_attn("owner_f", [1, ROUTED])
        early.close()

        wgu = [sb(f"wgu{h}", [P, 2, 2 * KT, D // 2], F32R) for h in range(2)]
        wdn = [sb(f"wdn{h}", [P, 2, KD // 2, H], F32R) for h in range(2)]
        xin = sb("xin", [P, 2, QT, RW])
        tx = [sb(f"tx{n}", [P, 2, KT, R], F32R) for n in range(2)]
        meta = sb("meta", [P, 2, QT, 2])
        hid = sb("hid", [P, 2, 2 * R])
        hs = [sb(f"hs{h}", [P, 2, KD // 2, R], F32R) for h in range(2)]
        ys = sb("ys", [P, 2, QT, H])
        raw = sb("raw", [P, E + 1, RAW])

        s_x = sem("s_x")
        s_c = sem("s_c")
        s_g = sem("s_g")
        s_b = sem("s_b")
        s_w = [sem(f"s_w{n}") for n in range(4)]
        ident_ready = sem("ident_ready")
        const_ready = sem("const_ready")
        zero_ready = sem("zero_ready")
        tanh_ready = sem("tanh_ready")
        bias_ready = sem("bias_ready")
        whi_ready = sem("whi_ready")
        wlo_ready = sem("wlo_ready")
        stat_step = sem("stat_step")
        stat_ready = sem("stat_ready")
        stat_passed = sem("stat_passed")
        var_passed = sem("var_passed")
        rstd_step = sem("rstd_step")
        rstd_ready = sem("rstd_ready")
        xn_ready = sem("xn_ready")
        ctx_ready = sem("ctx_ready")
        biased = sem("biased")
        xT_done, xT_hi, xT_lo = sem("xT_done"), sem("xT_hi"), sem("xT_lo")
        cT_done, cT_hi, cT_lo = sem("cT_done"), sem("cT_hi"), sem("cT_lo")
        q_done, q_hi, q_lo = sem("q_done"), sem("q_hi"), sem("q_lo")
        k_done, k_hi, k_lo = sem("k_done"), sem("k_hi"), sem("k_lo")
        v_done, v_hi, v_lo = sem("v_done"), sem("v_hi"), sem("v_lo")
        s_done = sem("s_done")
        max_ready, sub_ready, exp_ready = sem("max_ready"), sem("sub_ready"), sem("exp_ready")
        den_ready, rden_ready, norm_ready = sem("den_ready"), sem("rden_ready"), sem("norm_ready")
        p_done, p_hi, p_lo = sem("p_done"), sem("p_hi"), sem("p_lo")
        o_done, o_hi, o_lo = sem("o_done"), sem("o_hi"), sem("o_lo")
        y_done, y_added = sem("y_done"), sem("y_added")
        s_rows = sem("s_rows")
        s_pad = sem("s_pad")
        s_zero = sem("s_zero")
        s_linear = sem("s_linear")
        s_raw = [sem(f"s_raw{e}") for e in range(E + 1)]
        s_slots = sem("s_slots")
        x_loaded = [sem(f"x_loaded{n}") for n in range(2)]
        s_added = sem("s_added")
        pad_ready, id_ready, w_ready, wcol_ready = sem("pad_ready"), sem("id_ready"), sem("w_ready"), sem("wcol_ready")
        s_gw, gw_hi, gw_lo = sem("s_gw"), sem("gw_hi"), sem("gw_lo")
        stat2_step, stat2_ready, stat2_passed = sem("stat2_step"), sem("stat2_ready"), sem("stat2_passed")
        var2_passed, rstd2_step, rstd2_ready = sem("var2_passed"), sem("rstd2_step"), sem("rstd2_ready")
        xn2_ready, row0_ready, row1_ready = sem("xn2_ready"), sem("row0_ready"), sem("row1_ready")
        x2_done, x2_hi, x2_lo = sem("x2_done"), sem("x2_hi"), sem("x2_lo")
        l_done, l_ready = sem("l_done"), sem("l_ready")
        route_step = sem("route_step")
        shifted, expd = sem("shifted"), sem("expd")
        mask_ready, prefix_done = sem("mask_ready"), sem("prefix_done")
        pos_ready, etab_ready = sem("pos_ready"), sem("etab_ready")
        tx_done, tx_hi, tx_lo = sem("tx_done"), sem("tx_hi"), sem("tx_lo")
        gu_done, silu_ready, h_ready = sem("gu_done"), sem("silu_ready"), sem("h_ready")
        h_hi, h_lo = sem("h_hi"), sem("h_lo")
        d_done, y_ready = sem("d_done"), sem("y_ready")
        w_hi = [sem(f"w_hi{g}") for g in range(4)]
        w_lo = [sem(f"w_lo{g}") for g in range(4)]
        meta_ready, pool_passed = sem("meta_ready"), sem("pool_passed")

        def f32(ap):
            return ap.bitcast(F32)

        def flat(ap):
            return ap.rearrange("p a b -> p (a b)")

        def group_raw(e, g):
            w = raw[:, bass.ds(e, 1)].squeeze(1)
            if g < 2:
                return w[:, 0:GW].rearrange("p (a n) -> p a n", n=D)[:, :, g * (D // 2):(g + 1) * (D // 2)]
            n = KD // 2 * H
            return w[:, GW + (g - 2) * n:GW + (g - 1) * n].rearrange("p (a n) -> p a n", n=H)

        def group_split(g, part):
            return (wgu[g] if g < 2 else wdn[g - 2])[:, part]

        def expert(eng, t):
            return eng.value_load(etab[0:1, bass.ds(t, 1)], min_val=0, max_val=E)

        def over_tiles(eng, step, routed_from_here):
            step(0, 0)
            step(1, 1)
            with eng.Fori(1, SHARED // 2 - 1) as u:
                step(u * 2, 0)
                step(u * 2 + 1, 1)
            routed_from_here()
            with eng.Fori(SHARED // 2 - 1, TILES // 2 - 1) as u:
                step(u * 2, 0)
                step(u * 2 + 1, 1)
            step(TILES - 2, 0)
            step(TILES - 1, 1)

        def exists(t):
            return not isinstance(t, int) or t < TILES

        block = es.enter_context(nc.Block())

        @block.sync
        def _(sp):
            def load_expert(sp, e):
                gate, up, down = (w_gate[e], w_up[e], w_down[e]) if e < E else (ws_gate, ws_up, ws_down)
                for n, w in enumerate((gate, up)):
                    sp.dma_start(raw[:, e, n * KT * D:(n + 1) * KT * D].rearrange("p (k d) -> p k d", d=D),
                                 w.rearrange("(k p) d -> p k d", p=P)).then_inc(s_raw[e], 16)
                sp.dma_start(raw[:, e, GW:RAW].rearrange("p (m h) -> p m h", h=H),
                             down.rearrange("(m p) h -> p m h", p=P)).then_inc(s_raw[e], 16)

            sp.dma_start(rows[:], x.rearrange("b (j p) h -> p (b j) h", p=P)).then_inc(s_x, 16)
            sp.dma_start(crow[:], ctx_in.rearrange("b m c -> m b c")).then_inc(s_c, 16)
            for n, (w, k) in enumerate(((wq, KT), (wk, CT), (wv, CT), (wo, MT))):
                if n >= 2:
                    sp.wait_ge(whi_ready, n - 1)
                    sp.wait_ge(wlo_ready, n - 1)
                part = w.shape[0] // k
                sp.dma_start(wstage[0:part, n % 2].rearrange("p (k n) -> p k n", k=k),
                             w.rearrange("(k p) n -> p k n", k=k)).then_inc(s_w[n], 16)
            for e in range(E, EARLY - 1, -1):
                load_expert(sp, e)
            sp.dma_start(gw_raw[:], gate_w.rearrange("(k p) e -> p k e", p=P)).then_inc(s_gw, 16)
            sp.wait_ge(pad_ready, 2)
            with sp.Fori(0, ROUTED) as t:
                sp.dma_start(xg[bass.ds(t * R + N, R)].rearrange("(j p) c -> p j c", p=P), pad[:]).then_inc(s_pad, 16)
            sp.dma_start(out[N:N + R].rearrange("(j p) h -> p j h", p=P), pad[:, :, 0:H]).then_inc(s_zero, 16)
            sp.wait_ge(y_added, B)
            sp.dma_start(out[0:N].rearrange("(t p) h -> p t h", p=P), rows[:]).then_inc(s_rows, 16)
            sp.wait_ge(row0_ready, B)
            sp.wait_ge(wcol_ready, 1)
            sp.wait_ge(id_ready, 2)
            sp.dma_start(xg[0:N].rearrange("(t p) c -> p t c", p=P), xr[0][:]).then_inc(s_linear, 16)
            sp.wait_ge(s_rows, 16)
            for e in range(EARLY - 1, -1, -1):
                load_expert(sp, e)
            sp.wait_ge(s_linear, 16)

            def load_tile(t, p):
                sp.dma_start(xin[:, p], xg[bass.ds(t * R, R)].rearrange("(j q) c -> q j c", q=P)) \
                    .then_inc(x_loaded[p], 16)

            def refill(t, p):
                if not exists(t + 2):
                    return
                sp.wait_ge(tx_done, t + 1)
                sp.wait_ge(meta_ready, t + 1)
                load_tile(t + 2, p)

            def all_slots():
                sp.wait_ge(s_slots, 16 * TOP * T)

            load_tile(0, 0)
            load_tile(1, 1)
            over_tiles(sp, refill, all_slots)
            sp.wait_ge(s_added, 16 * QT * TILES)

        @block.gpsimd
        def _(pool):
            nc.gpsimd.memset(ident[:], 0.0).then_inc(const_ready, 1)
            nc.gpsimd.memset(half[:], -0.5).then_inc(const_ready, 1)
            pool.wait_ge(const_ready, 2)
            nc.gpsimd.affine_select(out=ident[:], in_=ident[:], compare_op=ALU.not_equal, fill=1.0,
                                    base=0, pattern=[[-1, P]], channel_multiplier=1).then_inc(ident_ready, 1)
            pool.dma_start(gx[:, 0:1], g_xattn.partition_broadcast(P)).then_inc(s_g, 16)
            pool.dma_start(gx[:, 1:2], g_ffn.partition_broadcast(P)).then_inc(s_g, 16)
            pool.dma_start(bias[:], bout.partition_broadcast(P)).then_inc(s_b, 16)
            nc.gpsimd.memset(f32(vz[:]), 0.0).then_inc(zero_ready, 1)
            nc.gpsimd.memset(pad[:], 0.0).then_inc(pad_ready, 1)
            pool.wait_ge(pad_ready, 1)
            nc.gpsimd.iota(pad[:, :, IDC].bitcast(I32), pattern=[[P, QT]], base=N, channel_multiplier=1) \
                .then_inc(pad_ready, 1)
            for k in range(TOP):
                nc.gpsimd.iota(xr[k][:, :, IDC].bitcast(I32), pattern=[[P, T]], base=0, channel_multiplier=1) \
                    .then_inc(id_ready, 1)
            pool.wait_ge(s_b, 16)
            pool.wait_ge(tanh_ready, 1)
            nc.gpsimd.tensor_scalar(bias[:], bias[:], tg[:, 0:1], None, ALU.mult).then_inc(bias_ready, 1)
            pool.wait_ge(bias_ready, 1)

            def prepare(n):
                pool.wait_ge(s_c, 16)
                pool.wait_ge(cT_done, n)
                nc.gpsimd.tensor_copy(cbuf[:], crow[:, bass.ds(n, 1)].squeeze(1)).then_inc(ctx_ready, 1)
                pool.wait_ge(stat_ready, n + 1)
                pool.sem_inc(var_passed, 1)
                nc.gpsimd.tensor_scalar(vare[:], mv[:, :, 1], EPS, None, ALU.add).then_inc(rstd_step, 1)
                pool.wait_ge(rstd_step, n + 1)
                nc.gpsimd.tensor_tensor(rstd[:], vare[:], half[:], ALU.pow).then_inc(rstd_ready, 1)

            def prepare2(n):
                pool.wait_ge(stat2_ready, n + 1)
                pool.sem_inc(pool_passed, 1)
                nc.gpsimd.tensor_scalar(vare2[:], mv2[:, :, 1], EPS, None, ALU.add).then_inc(rstd2_step, 1)
                pool.wait_ge(rstd2_step, n + 1)
                nc.gpsimd.tensor_tensor(rstd2[:], vare2[:], half[:], ALU.pow).then_inc(rstd2_ready, 1)

            def keep_rows(n):
                pool.wait_ge(xn2_ready, n + 1)
                nc.gpsimd.tensor_copy(xr[1][:, bass.ds(n * QT, QT), 0:H], xn2[:]).then_inc(row1_ready, 1)

            def normalise(b):
                for j in range(QT):
                    pool.wait_ge(rden_ready, QT * b + j + 1)
                    pr = prob[:, j].rearrange("p a m k -> p (a m) k")
                    nc.gpsimd.tensor_tensor(pr, pr, rden[:, j].rearrange("p a m -> p (a m)").unsqueeze(2)
                                            .to_broadcast([P, HEADS, M]), ALU.mult).then_inc(norm_ready, 1)

            def add_bias(b):
                pool.wait_ge(xn_ready, b + 1)
                r = rows[:, bass.ds(b * QT, QT)]
                nc.gpsimd.tensor_tensor(r, r, bias[:].unsqueeze(1).to_broadcast([P, QT, H]),
                                        ALU.add).then_inc(biased, 1)

            def step(b, first, last):
                if not first:
                    prepare2(b - 1)
                if not last:
                    prepare(b + 1)
                add_bias(b)
                normalise(b)
                if not first:
                    keep_rows(b - 1)

            prepare(0)
            step(0, True, False)
            with pool.Fori(1, B - 1) as b:
                step(b, False, False)
            step(B - 1, False, True)
            prepare2(B - 1)
            keep_rows(B - 1)

            nc.gpsimd.memset(ones[:], 1.0).then_inc(const_ready, 1)
            for t in (less, more, before):
                nc.gpsimd.memset(t[:], 1.0).then_inc(const_ready, 1)
            nc.gpsimd.iota(count_i[:], pattern=[[1, ROUTED]], base=0, channel_multiplier=0).then_inc(const_ready, 1)
            nc.gpsimd.memset(etab[0:1, 0:SHARED], E).then_inc(const_ready, 1)
            pool.wait_ge(const_ready, 8)
            nc.gpsimd.affine_select(out=less[:], in_=less[:], compare_op=ALU.is_gt, fill=0.0, base=0,
                                    pattern=[[1, E], [-1, E]], channel_multiplier=0).then_inc(const_ready, 1)
            nc.gpsimd.affine_select(out=more[:], in_=more[:], compare_op=ALU.is_gt, fill=0.0, base=0,
                                    pattern=[[-1, E], [1, E]], channel_multiplier=0).then_inc(const_ready, 1)
            nc.gpsimd.affine_select(out=before[:], in_=before[:], compare_op=ALU.is_gt, fill=0.0, base=0,
                                    pattern=[[1, P]], channel_multiplier=-1).then_inc(const_ready, 1)

            pool.wait_ge(pos_ready, 1)
            pool.wait_ge(s_pad, 16 * ROUTED)
            for j in range(T):
                for k in range(TOP):
                    pool.indirect_dma_start(out=xg, out_offset=bass.IndirectOffsetOnAxis(ap=pos[:, k, j:j + 1], axis=0),
                                            in_=xr[k][:, j, :], in_offset=None).then_inc(s_slots, 16)

            def split_low(t, g, e):
                pool.wait_ge(w_hi[g], t + 1)
                nc.gpsimd.tensor_tensor(group_split(g, LO), group_raw(e, g), f32(group_split(g, HI)),
                                        ALU.subtract).then_inc(w_lo[g], 1)

            def copy_meta(t, p):
                pool.wait_ge(x_loaded[p], (t // 2 + 1) * 16 if isinstance(t, int) else t * 8 + (16 - 8 * p))
                pool.sem_inc(pool_passed, 1)
                nc.gpsimd.tensor_copy(meta[:, p], xin[:, p, :, IDC:RW]).then_inc(meta_ready, 1)

            def tile(t, p):
                e1 = expert(pool, t + 1) if exists(t + 1) else None
                if exists(t + 1):
                    split_low(t + 1, 1, e1)
                    split_low(t + 1, 2, e1)
                pool.wait_ge(s_added, t * (16 * QT))
                pool.sem_inc(pool_passed, 1)
                if exists(t + 1):
                    copy_meta(t + 1, 1 - p)
                    split_low(t + 1, 3, e1)
                pool.wait_ge(y_ready, t + 1)
                pool.sem_inc(pool_passed, 1)
                for j in range(QT):
                    pool.indirect_dma_start(
                        out=out, out_offset=bass.IndirectOffsetOnAxis(ap=meta[:, p, j, 0:1].bitcast(U32), axis=0),
                        in_=ys[:, p, j], in_offset=None, compute_op=ALU.add).then_inc(s_added, 16)

            pool.wait_ge(etab_ready, 1)
            pool.wait_ge(s_rows, 16)
            pool.wait_ge(s_zero, 16)
            for g in (1, 2, 3):
                split_low(0, g, expert(pool, 0))
            copy_meta(0, 0)
            over_tiles(pool, tile, lambda: None)

        @block.scalar
        def _(act):
            act.wait_ge(s_g, 32)
            nc.scalar.activation(tg[:], gx[:], ACT.Tanh).then_inc(tanh_ready, 1)
            for n, (w, part) in enumerate(((wq_s, P), (wk_s, CP), (wv_s, CP), (wo_s, P))):
                act.wait_ge(s_w[n], 16)
                nc.scalar.copy(w[:, HI].rearrange("p k n -> p (k n)"), wstage[0:part, n % 2]).then_inc(whi_ready, 1)

            def transposed(n):
                act.wait_ge(xT_done, n + 1)
                nc.scalar.copy(xT[:, HI].rearrange("p k s -> p (k s)"), BD).then_inc(xT_hi, 1)
                act.wait_ge(cT_done, n + 1)
                nc.scalar.copy(cT[:, HI].rearrange("p k s -> p (k s)"), BE[0:CP, 0:CT * M]).then_inc(cT_hi, 1)

            def projected(n):
                for i, bank in ((0, BC1), (1, BC0)):
                    act.wait_ge(q_done, 2 * n + i + 1)
                    nc.scalar.mul(qT[:, HI, 2 * i:2 * i + 2].rearrange("p k s -> p (k s)"), bank, SCALE) \
                        .then_inc(q_hi, 1)
                act.wait_ge(k_done, n + 1)
                nc.scalar.copy(kT[:, HI].rearrange("p k s -> p (k s)"), BD[:, 0:MT * M]).then_inc(k_hi, 1)

            def exp(b, j):
                act.wait_ge(sub_ready, QT * b + j + 1)
                nc.scalar.activation(prob[:, j], prob[:, j], ACT.Exp).then_inc(exp_ready, 1)

            def values(b):
                act.wait_ge(v_done, b + 1)
                act.wait_ge(zero_ready, 1)
                v = vz[:, HI].rearrange("p (g a) (c d) -> p g (a c) d", a=2, c=2)[:, :, 0:4:3]
                nc.scalar.copy(v, BC0[0:M].rearrange("p (g a d) -> p g a d", g=PAIRS, a=2)).then_inc(v_hi, 1)

            def attended(b):
                for i in range(2):
                    act.wait_ge(p_done, 2 * b + i + 1)
                    nc.scalar.copy(pT[:, HI, 4 * i:4 * i + 4].rearrange("p (c h) s -> p c (h s)", c=2),
                                   SCORES[i][0:M]).then_inc(p_hi, 1)
                for i, bank in ((0, BE), (1, BC1)):
                    act.wait_ge(o_done, 2 * b + i + 1)
                    nc.scalar.copy(oT[:, HI, 2 * i:2 * i + 2].rearrange("p k s -> p (k s)"), bank).then_inc(o_hi, 1)

            def normed(n):
                act.wait_ge(xn2_ready, n + 1)
                nc.scalar.copy(xr[0][:, bass.ds(n * QT, QT), 0:H], xn2[:]).then_inc(row0_ready, 1)
                act.wait_ge(x2_done, n + 1)
                nc.scalar.copy(flat(x2T[:, HI]), BE).then_inc(x2_hi, 1)

            def step(b, first, last):
                exp(b, 0)
                values(b)
                exp(b, 1)
                if not first:
                    normed(b - 1)
                if not last:
                    transposed(b + 1)
                    projected(b + 1)
                attended(b)

            transposed(0)
            projected(0)
            act.wait_ge(s_gw, 16)
            nc.scalar.copy(gw_s[:, HI], gw_raw[:]).then_inc(gw_hi, 1)
            step(0, True, False)
            with act.Fori(1, B - 1) as b:
                step(b, False, False)
            step(B - 1, False, True)
            normed(B - 1)

            act.wait_ge(shifted, 1)
            nc.scalar.activation(score[:], rank[:], ACT.Exp).then_inc(expd, 1)

            def split_high(t, g, e):
                nc.scalar.copy(group_split(g, HI), group_raw(e, g)).then_inc(w_hi[g], 1)

            def rows_high(t, p):
                act.wait_ge(tx_done, t + 1)
                nc.scalar.copy(flat(tx[p][:, HI]), TXB).then_inc(tx_hi, 1)

            def silu(t, h):
                act.wait_ge(gu_done, t * 2 + h + 1)
                nc.scalar.activation(hid[:, h], GATE[h], ACT.Silu).then_inc(silu_ready, 1)

            def hidden_high(t, h):
                act.wait_ge(h_ready, t * 2 + h + 1)
                nc.scalar.copy(flat(hs[h][:, HI]), hid[:, h]).then_inc(h_hi, 1)

            def tile(t, p):
                e1 = expert(act, t + 1) if exists(t + 1) else None
                e2 = expert(act, t + 2) if exists(t + 2) else None
                if exists(t + 1):
                    rows_high(t + 1, 1 - p)
                silu(t, 1)
                if exists(t + 1):
                    split_high(t + 1, 1, e1)
                hidden_high(t, 1)
                if exists(t + 1):
                    act.wait_ge(d_done, t * 2 + 1)
                    split_high(t + 1, 2, e1)
                    silu(t + 1, 0)
                    if exists(t + 2):
                        split_high(t + 2, 0, e2)
                    hidden_high(t + 1, 0)
                    act.wait_ge(d_done, t * 2 + 2)
                    split_high(t + 1, 3, e1)

            act.wait_ge(etab_ready, 1)
            act.wait_ge(s_raw[E], 48)
            act.wait_ge(s_rows, 16)
            for g in range(4):
                split_high(0, g, expert(act, 0))
            rows_high(0, 0)
            silu(0, 0)
            split_high(1, 0, expert(act, 1))
            hidden_high(0, 0)

            def all_weights():
                for e in range(E):
                    act.wait_ge(s_raw[e], 48)
            over_tiles(act, tile, all_weights)

        @block.vector
        def _(dve):
            for n, (w, part) in enumerate(((wq_s, P), (wk_s, CP), (wv_s, CP), (wo_s, P))):
                dve.wait_ge(whi_ready, n + 1)
                nc.vector.tensor_tensor(w[:, LO].rearrange("p k n -> p (k n)"), wstage[0:part, n % 2],
                                        f32(w[:, HI]).rearrange("p k n -> p (k n)"),
                                        ALU.subtract).then_inc(wlo_ready, 1)

            def low(dst, src, hi, done):
                nc.vector.tensor_tensor(dst, src, hi, ALU.subtract).then_inc(done, 1)

            def statistics(n):
                for j in range(QT):
                    nc.vector.bn_stats(stats[:, j], rows[:, bass.ds(n * QT + j, 1)].squeeze(1)).then_inc(stat_step, 1)
                dve.wait_ge(stat_step, QT * n + QT)
                dve.sem_inc(stat_passed, 1)
                for j in range(QT):
                    i = nc.vector.bn_aggr(mv[:, j], stats[:, j])
                i.then_inc(stat_ready, 1)

            def layer_norm(n):
                dve.wait_ge(stat_ready, n + 1)
                dve.wait_ge(rstd_ready, n + 1)
                dve.wait_ge(xT_done, n)
                for j in range(QT):
                    i = nc.vector.tensor_scalar(xn[:, j], rows[:, bass.ds(n * QT + j, 1)].squeeze(1), mv[:, j, 0:1],
                                                rstd[:, j:j + 1], ALU.subtract, ALU.mult)
                i.then_inc(xn_ready, 1)

            def transposed(n):
                dve.wait_ge(xT_hi, n + 1)
                low(xT[:, LO].rearrange("p k s -> p (k s)"), BD, f32(xT[:, HI]).rearrange("p k s -> p (k s)"), xT_lo)
                dve.wait_ge(cT_hi, n + 1)
                low(cT[:, LO].rearrange("p k s -> p (k s)"), BE[0:CP, 0:CT * M],
                    f32(cT[:, HI]).rearrange("p k s -> p (k s)"), cT_lo)

            def projected(n):
                for i, bank in ((0, BC1), (1, BC0)):
                    dve.wait_ge(q_hi, 2 * n + i + 1)
                    part = slice(2 * i, 2 * i + 2)
                    nc.vector.scalar_tensor_tensor(
                        out=qT[:, LO, part].rearrange("p k s -> p (k s)"), in0=bank, scalar=SCALE,
                        in1=f32(qT[:, HI, part]).rearrange("p k s -> p (k s)"), op0=ALU.mult,
                        op1=ALU.subtract).then_inc(q_lo, 1)
                dve.wait_ge(k_hi, n + 1)
                low(kT[:, LO].rearrange("p k s -> p (k s)"), BD[:, 0:MT * M],
                    f32(kT[:, HI]).rearrange("p k s -> p (k s)"), k_lo)

            def maximum(b, j):
                dve.wait_ge(s_done, QT * b + j + 1)
                sc = SCORES[j][:, :, 0:PAIRS * M].rearrange("p a (m k) -> p a m k", k=M)
                nc.vector.tensor_reduce(mx[:, j], sc, AX.X, ALU.max).then_inc(max_ready, 1)
                dve.wait_ge(max_ready, QT * b + j + 1)
                dve.wait_ge(p_done, 2 * b)
                for a in range(2):
                    i = nc.vector.tensor_tensor(prob[:, j, a], sc[:, a],
                                                mx[:, j, a].unsqueeze(2).to_broadcast([P, PAIRS, M]), ALU.subtract)
                i.then_inc(sub_ready, 1)

            def denominator(b, j):
                dve.wait_ge(exp_ready, QT * b + j + 1)
                nc.vector.tensor_reduce(den[:, j], prob[:, j], AX.X, ALU.add).then_inc(den_ready, 1)
                dve.wait_ge(den_ready, QT * b + j + 1)
                nc.vector.reciprocal(rden[:, j], den[:, j]).then_inc(rden_ready, 1)

            def values(b):
                dve.wait_ge(v_hi, b + 1)
                v = [vz[:, w].rearrange("p (g a) (c d) -> p g (a c) d", a=2, c=2)[:, :, 0:4:3] for w in (HI, LO)]
                low(v[LO], BC0[0:M].rearrange("p (g a d) -> p g a d", g=PAIRS, a=2), f32(v[HI]), v_lo)

            def attended(b):
                for i in range(2):
                    dve.wait_ge(p_hi, 2 * b + i + 1)
                    q = [pT[:, w, 4 * i:4 * i + 4].rearrange("p (c h) s -> p c (h s)", c=2) for w in (HI, LO)]
                    low(q[LO], SCORES[i][0:M], f32(q[HI]), p_lo)
                for i, bank in ((0, BE), (1, BC1)):
                    dve.wait_ge(o_hi, 2 * b + i + 1)
                    part = slice(2 * i, 2 * i + 2)
                    low(oT[:, LO, part].rearrange("p k s -> p (k s)"), bank,
                        f32(oT[:, HI, part]).rearrange("p k s -> p (k s)"), o_lo)
                dve.wait_ge(y_done, b + 1)
                dve.wait_ge(biased, b + 1)
                r = rows[:, bass.ds(b * QT, QT)].rearrange("p j h -> p (j h)")
                nc.vector.scalar_tensor_tensor(out=r, in0=BC0, scalar=tg[:, 0:1], in1=r, op0=ALU.mult,
                                               op1=ALU.add).then_inc(y_added, 1)

            def statistics2(n):
                dve.wait_ge(y_added, n + 1)
                dve.sem_inc(stat2_passed, 1)
                for j in range(QT):
                    nc.vector.bn_stats(stats2[:, j], rows[:, bass.ds(n * QT + j, 1)].squeeze(1)).then_inc(stat2_step, 1)
                dve.wait_ge(stat2_step, QT * n + QT)
                dve.sem_inc(stat2_passed, 1)
                for j in range(QT):
                    i = nc.vector.bn_aggr(mv2[:, j], stats2[:, j])
                i.then_inc(stat2_ready, 1)

            def layer_norm2(n):
                dve.wait_ge(stat2_ready, n + 1)
                dve.wait_ge(rstd2_ready, n + 1)
                for j in range(QT):
                    i = nc.vector.tensor_scalar(xn2[:, j], rows[:, bass.ds(n * QT + j, 1)].squeeze(1), mv2[:, j, 0:1],
                                                rstd2[:, j:j + 1], ALU.subtract, ALU.mult)
                i.then_inc(xn2_ready, 1)

            def normed(n):
                dve.wait_ge(x2_hi, n + 1)
                low(flat(x2T[:, LO]), BE, flat(f32(x2T[:, HI])), x2_lo)

            def logits(n):
                dve.wait_ge(l_done, n + 1)
                nc.vector.tensor_copy(logit[:, bass.ds(n * QT, QT)], BE[:, 0:QT * E].rearrange("p (j e) -> p j e", e=E)) \
                    .then_inc(l_ready, 1)

            def step(b, first, last):
                if not first:
                    statistics2(b - 1)
                maximum(b, 0)
                if not last:
                    layer_norm(b + 1)
                if not first:
                    layer_norm2(b - 1)
                maximum(b, 1)
                values(b)
                denominator(b, 0)
                if not first:
                    normed(b - 1)
                if not last:
                    transposed(b + 1)
                denominator(b, 1)
                if not last:
                    projected(b + 1)
                if not first:
                    logits(b - 1)
                attended(b)

            dve.wait_ge(s_x, 16)
            statistics(0)
            layer_norm(0)
            transposed(0)
            projected(0)
            statistics(1)
            dve.wait_ge(tanh_ready, 1)
            nc.vector.tensor_copy(xr[0][:, :, WC], tg[:, 1:2].to_broadcast([P, T])).then_inc(wcol_ready, 1)
            dve.wait_ge(gw_hi, 1)
            low(gw_s[:, LO], gw_raw[:], f32(gw_s[:, HI]), gw_lo)
            step(0, True, False)
            statistics(2)
            with dve.Fori(1, B - 2) as b:
                step(b, False, False)
                statistics(b + 2)
            step(B - 2, False, False)
            step(B - 1, False, True)
            statistics2(B - 1)
            layer_norm2(B - 1)
            normed(B - 1)
            logits(B - 1)

            steps = [0]

            def then(i):
                steps[0] += 1
                i.then_inc(route_step, 1)
                dve.wait_ge(route_step, steps[0])

            V = nc.vector
            s0, s1, s2, s3, s4, s5 = (t[:] for t in small)

            def over_e(ap):
                return ap.unsqueeze(2).to_broadcast([P, T, E])

            dve.wait_ge(const_ready, 11)
            dve.wait_ge(l_ready, B)
            V.tensor_copy(count[:], count_i[:])
            then(V.tensor_reduce(s0, logit[:], AX.X, ALU.max))
            V.tensor_tensor(rank[:], logit[:], over_e(s0), ALU.subtract).then_inc(shifted, 1)
            then(V.tensor_scalar(count_r[:], count[:, 0:E], float(R), None, ALU.mult))
            dve.wait_ge(expd, 1)
            then(V.tensor_reduce(s1, score[:], AX.X, ALU.add))
            then(V.reciprocal(s2, s1))
            then(V.tensor_tensor(score[:], score[:], over_e(s2), ALU.mult))
            wide = [t[:].rearrange("p a b c -> p (a b c)") if len(t.shape) == 4 else flat(t[:]) for t in (ys, hid)]
            higher, equal = (w.rearrange("p (t e j) -> p t e j", t=T, e=E) for w in wide)
            other = score[:].unsqueeze(2).to_broadcast([P, T, E, E])
            own = score[:].unsqueeze(3).to_broadcast([P, T, E, E])
            V.tensor_tensor(higher, other, own, ALU.is_gt)
            then(V.tensor_tensor(equal, other, own, ALU.is_equal))
            then(V.tensor_tensor(equal, equal, less[:].unsqueeze(1).to_broadcast([P, T, E, E]), ALU.mult))
            then(V.tensor_tensor(higher, higher, equal, ALU.add))
            then(V.tensor_reduce(rank[:], higher, AX.X, ALU.add))
            for k in range(TOP):
                V.tensor_scalar(sel[k][:], rank[:], float(k), None, ALU.is_equal)
            then(V.tensor_scalar(mask[:], rank[:], float(TOP), None, ALU.is_lt))
            i = V.tensor_tensor(picked[:], sel[0][:], score[:], ALU.mult)
            i.then_inc(mask_ready, 1)
            dve.wait_ge(mask_ready, 1)
            then(V.tensor_reduce(s0, picked[:], AX.X, ALU.add))
            then(V.tensor_tensor(picked[:], sel[1][:], score[:], ALU.mult))
            then(V.tensor_reduce(s1, picked[:], AX.X, ALU.add))
            then(V.tensor_tensor(s2, s0, s1, ALU.add))
            then(V.tensor_scalar(s3, s2, 1e-20, None, ALU.add))
            then(V.reciprocal(s4, s3))
            then(V.tensor_scalar(s5, s4, tg[:, 1:2], None, ALU.mult))
            dve.wait_ge(s_linear, 16)
            V.tensor_tensor(xr[0][:, :, WC], s0, s5, ALU.mult)
            then(V.tensor_tensor(xr[1][:, :, WC], s1, s5, ALU.mult))
            dve.wait_ge(prefix_done, 1)
            V.tensor_copy(inside[:].rearrange("p t e -> p (t e)"), BD[:, 0:T * E])
            then(V.tensor_copy(total[:].rearrange("p t e -> p (t e)"), BE[:, 0:T * E]))
            src = total
            for n, d in enumerate((1, 2, 4, 8)):
                dst = cum[n % 2]
                V.tensor_copy(dst[:, 0:d], src[:, 0:d])
                then(V.tensor_tensor(dst[:, d:T], src[:, d:T], src[:, 0:T - d], ALU.add))
                src = dst
            then(V.tensor_tensor(slot[:], src[:], total[:], ALU.subtract))
            then(V.tensor_tensor(slot[:], slot[:], inside[:], ALU.add))
            counted = src[:, T - 1]
            then(V.tensor_tensor(square[:], counted.unsqueeze(2).to_broadcast([P, E, E]),
                                 count_r[:].unsqueeze(1).to_broadcast([P, E, E]), ALU.is_gt))
            then(V.tensor_reduce(tiles_e[:], square[:], AX.X, ALU.add))
            then(V.tensor_tensor(square2[:], more[:], tiles_e[:].unsqueeze(1).to_broadcast([P, E, E]), ALU.mult))
            then(V.tensor_reduce(base_e[:], square2[:], AX.X, ALU.add))
            then(V.tensor_scalar(tiles_e[:], base_e[:], float(R), float(N), ALU.mult, ALU.add))
            then(V.tensor_tensor(slot[:], slot[:], tiles_e[:].unsqueeze(1).to_broadcast([P, T, E]), ALU.add))
            for k in range(TOP):
                then(V.tensor_tensor(picked[:], sel[k][:], slot[:], ALU.mult))
                then(V.tensor_reduce(small[k][:], picked[:], AX.X, ALU.add))
            V.tensor_copy(pos[:, 0], s0)
            V.tensor_copy(pos[:, 1], s1).then_inc(pos_ready, 1)
            then(V.tensor_tensor(owner[:], base_e[0:1].unsqueeze(1).to_broadcast([1, ROUTED, E]),
                                 count[0:1].unsqueeze(2).to_broadcast([1, ROUTED, E]), ALU.is_gt))
            then(V.tensor_reduce(owner_f[:], owner[:], AX.X, ALU.add))
            V.tensor_copy(etab[0:1, SHARED:TILES], owner_f[:]).then_inc(etab_ready, 1)

            def rows_low(t, p):
                dve.wait_ge(tx_hi, t + 1)
                low(flat(tx[p][:, LO]), TXB, flat(f32(tx[p][:, HI])), tx_lo)

            def split_low(t, g, e):
                dve.wait_ge(w_hi[g], t + 1)
                low(group_split(g, LO), group_raw(e, g), f32(group_split(g, HI)), w_lo[g])

            def hidden(t, h):
                dve.wait_ge(silu_ready, t * 2 + h + 1)
                V.tensor_tensor(hid[:, h], hid[:, h], UP[h], ALU.mult).then_inc(h_ready, 1)

            def hidden_low(t, h):
                dve.wait_ge(h_hi, t * 2 + h + 1)
                low(flat(hs[h][:, LO]), hid[:, h], flat(f32(hs[h][:, HI])), h_lo)

            def weigh(t, p):
                dve.wait_ge(d_done, t * 2 + 2)
                dve.wait_ge(meta_ready, t + 1)
                if not isinstance(t, int) or t >= 2:
                    dve.wait_ge(s_added, t * (16 * QT) - 16 * QT)
                for j in range(QT):
                    i = V.tensor_scalar(ys[:, p, j], YB[j], meta[:, p, j, 1:2], None, ALU.mult)
                i.then_inc(y_ready, 1)

            def tile(t, p):
                e2 = expert(dve, t + 2) if exists(t + 2) else None
                if exists(t + 1):
                    rows_low(t + 1, 1 - p)
                hidden(t, 1)
                hidden_low(t, 1)
                if exists(t + 1):
                    hidden(t + 1, 0)
                    if exists(t + 2):
                        split_low(t + 2, 0, e2)
                    hidden_low(t + 1, 0)
                weigh(t, p)

            dve.wait_ge(etab_ready, 1)
            split_low(0, 0, expert(dve, 0))
            rows_low(0, 0)
            hidden(0, 0)
            split_low(1, 0, expert(dve, 1))
            hidden_low(0, 0)
            over_tiles(dve, tile, lambda: None)

        @block.tensor
        def _(pe):
            pe.wait_ge(ident_ready, 1)
            pe.wait_ge(wlo_ready, 4)

            def transposes(n):
                pe.wait_ge(xn_ready, n + 1)
                pe.wait_ge(k_lo, n)
                for k in range(KT):
                    for j in range(QT):
                        i = nc.tensor.transpose(BD[:, k * S + j * P:k * S + j * P + P], xn[:, j, k * P:(k + 1) * P],
                                                ident[:])
                i.then_inc(xT_done, 1)
                pe.wait_ge(ctx_ready, n + 1)
                for k in range(CT):
                    i = nc.tensor.transpose(BE[0:CP, k * M:(k + 1) * M], cbuf[:, k * CP:(k + 1) * CP],
                                            ident[0:M, 0:M])
                i.then_inc(cT_done, 1)

            def product(dst, lhs, rhs, ks):
                for n, k in enumerate(ks):
                    for u, (a, c) in enumerate(PASSES):
                        i = nc.tensor.matmul(dst, lhs(a, k), rhs(c, k), start=(n == 0 and u == 0),
                                             stop=(n == len(ks) - 1 and u == 2))
                return i

            def projections(n):
                pe.wait_ge(xT_lo, n + 1)
                for h, bank in ((0, BC1), (1, BC0)):
                    if h == 1:
                        pe.wait_ge(v_lo, n)
                    for m in range(2):
                        mt = 2 * h + m
                        i = product(bank[:, m * S:(m + 1) * S], lambda a, k: wq_s[:, a, k, mt * P:(mt + 1) * P],
                                    lambda a, k: xT[:, a, k], range(KT))
                    i.then_inc(q_done, 1)
                pe.wait_ge(cT_lo, n + 1)
                for m in range(MT):
                    i = product(BD[:, m * M:(m + 1) * M], lambda a, k: wk_s[:, a, k, m * P:(m + 1) * P],
                                lambda a, k: cT[:, a, k], range(CT))
                i.then_inc(k_done, 1)

            def scores(b):
                pe.wait_ge(q_lo, 2 * b + 2)
                pe.wait_ge(k_lo, b + 1)
                for j in range(QT):
                    pe.wait_ge(p_lo, 2 * b)
                    for m in range(PAIRS):
                        for u, (w, c) in enumerate(PASSES):
                            for a in range(2):
                                i = nc.tensor.matmul(SCORES[j][:, a, m * M:(m + 1) * M],
                                                     qT[a * DH:(a + 1) * DH, w, m, j * P:(j + 1) * P],
                                                     kT[a * DH:(a + 1) * DH, c, m, :], start=(u == 0), stop=(u == 2))
                    i.then_inc(s_done, 1)

            def values(b):
                pe.wait_ge(y_added, b)
                product(BC0[0:M], lambda a, k: cT[:, a, k], lambda a, k: wv_s[:, a, k], range(CT)) \
                    .then_inc(v_done, 1)

            def attend(b):
                pe.wait_ge(norm_ready, QT * b + QT)
                for i in range(2):
                    for hh in range(4):
                        h = 4 * i + hh
                        for j in range(QT):
                            t = nc.tensor.transpose(SCORES[i][0:M, hh // 2, (hh % 2) * S + j * P:(hh % 2) * S + j * P + P],
                                                    prob[:, j, h % 2, h // 2], ident[:])
                    t.then_inc(p_done, 1)
                pe.wait_ge(v_lo, b + 1)
                for i, bank in ((0, BE), (1, BC1)):
                    pe.wait_ge(p_lo, 2 * b + i + 1)
                    for g in range(2):
                        h = 4 * i + 2 * g
                        t = product(bank[:, g * S:(g + 1) * S], lambda a, k: vz[:, a, k],
                                    lambda a, k: pT[:, a, k], (h, h + 1))
                    t.then_inc(o_done, 1)
                pe.wait_ge(o_lo, 2 * b + 2)
                for j in range(QT):
                    t = product(BC0[:, j * H:(j + 1) * H], lambda a, k: oT[:, a, k, j * P:(j + 1) * P],
                                lambda a, k: wo_s[:, a, k], range(MT))
                t.then_inc(y_done, 1)

            def transposes2(n):
                pe.wait_ge(xn2_ready, n + 1)
                for k in range(KT):
                    for j in range(QT):
                        i = nc.tensor.transpose(BE[:, k * S + j * P:k * S + j * P + P], xn2[:, j, k * P:(k + 1) * P],
                                                ident[:])
                i.then_inc(x2_done, 1)

            def logits(n):
                pe.wait_ge(x2_lo, n + 1)
                pe.wait_ge(gw_lo, 1)
                for j in range(QT):
                    i = product(BE[:, j * E:(j + 1) * E], lambda a, k: x2T[:, a, k, j * P:(j + 1) * P],
                                lambda a, k: gw_s[:, a, k], range(KT))
                i.then_inc(l_done, 1)

            def step(b, first, last):
                scores(b)
                values(b)
                if not first:
                    transposes2(b - 1)
                if not last:
                    if not first:
                        pe.wait_ge(x2_lo, b)
                    transposes(b + 1)
                    projections(b + 1)
                if not first:
                    if not last:
                        pe.wait_ge(cT_lo, b + 2)
                    logits(b - 1)
                    pe.wait_ge(l_ready, b)
                attend(b)

            transposes(0)
            projections(0)
            step(0, True, False)
            with pe.Fori(1, B - 1) as b:
                step(b, False, False)
            step(B - 1, False, True)
            transposes2(B - 1)
            logits(B - 1)

            pe.wait_ge(mask_ready, 1)
            pe.wait_ge(l_ready, B)
            m = mask[:].rearrange("p t e -> p (t e)")
            nc.tensor.matmul(BD[:, 0:T * E], before[:], m, start=True, stop=True)
            nc.tensor.matmul(BE[:, 0:T * E], ones[:], m, start=True, stop=True).then_inc(prefix_done, 1)

            def rows_in(t, p):
                pe.wait_ge(x_loaded[p], (t // 2 + 1) * 16 if isinstance(t, int) else t * 8 + (16 - 8 * p))
                pe.wait_ge(tx_lo, t)
                for k in range(KT):
                    for j in range(QT):
                        i = nc.tensor.transpose(TXB[:, k * R + j * P:k * R + j * P + P], xin[:, p, j, k * P:(k + 1) * P],
                                                ident[:])
                i.then_inc(tx_done, 1)

            def gate_up(t, p, h):
                pe.wait_ge(w_lo[h], t + 1)
                pe.wait_ge(tx_lo, t + 1)
                if not isinstance(t, int) or t >= 1:
                    pe.wait_ge(h_ready, t * 2 + h - 1)
                for c, bank in ((0, GATE[h]), (1, UP[h])):
                    for m in range(KD // 2):
                        i = product(bank[:, m * R:(m + 1) * R],
                                    lambda a, k: wgu[h][:, a, c * KT + k, m * P:(m + 1) * P],
                                    lambda a, k: tx[p][:, a, k], range(KT))
                i.then_inc(gu_done, 1)

            def down(t, h):
                pe.wait_ge(w_lo[2 + h], t + 1)
                pe.wait_ge(h_lo, t * 2 + h + 1)
                if h == 0:
                    pe.wait_ge(y_ready, t)
                for j in range(QT):
                    for m in range(KD // 2):
                        for u, (a, c) in enumerate(PASSES):
                            i = nc.tensor.matmul(YB[j], hs[h][:, a, m, j * P:(j + 1) * P], wdn[h][:, c, m],
                                                 start=(h == 0 and m == 0 and u == 0),
                                                 stop=(h == 1 and m == KD // 2 - 1 and u == 2))
                i.then_inc(d_done, 1)

            def tile(t, p):
                if exists(t + 1):
                    rows_in(t + 1, 1 - p)
                gate_up(t, p, 1)
                down(t, 0)
                if exists(t + 1):
                    gate_up(t + 1, 1 - p, 0)
                down(t, 1)

            pe.wait_ge(etab_ready, 1)
            rows_in(0, 0)
            gate_up(0, 0, 0)
            over_tiles(pe, tile, lambda: None)


_INS = ['x', 'ctx_768', 'g_xattn', 'g_ffn', 'L0_xattn_Wq', 'L0_xattn_Wk', 'L0_xattn_Wv', 'L0_xattn_Wout',
        'L0_xattn_bout', 'L0_ffn_gate_w', 'L0_ffn_w_gate', 'L0_ffn_w_up', 'L0_ffn_w_down', 'L0_ffn_ws_gate',
        'L0_ffn_ws_up', 'L0_ffn_ws_down']
_OUT = (8, 256, 256)
_SPARE = 256


def kernel(**inputs):
    import numpy as _np
    import concourse.bacc as _bacc
    from concourse import mybir as _mybir
    from concourse.bass_utils import run_bass_kernel_spmd as _run

    nc = _bacc.Bacc("TRN2", target_bir_lowering=False, num_devices=1)
    arrays, args = {}, []
    for name in _INS:
        a = _np.ascontiguousarray(inputs[name])
        arrays[f"in_{name}_dram"] = a
        args.append(nc.dram_tensor(f"in_{name}_dram", a.shape, _mybir.dt.from_np(a.dtype), kind="ExternalInput").ap())
    out = nc.dram_tensor("out_dram", (_OUT[0] * _OUT[1] + _SPARE, _OUT[2]), _mybir.dt.float32, kind="ExternalOutput").ap()
    build(nc, *args, out)
    r = _run(nc, [arrays], core_ids=[0])
    return r.results[0]["out_dram"][:_OUT[0] * _OUT[1]].reshape(_OUT)
```

```python
from contextlib import ExitStack

import concourse.bass as bass
from concourse import mybir

F32 = mybir.dt.float32
F32R = mybir.dt.float32r
U32 = mybir.dt.uint32
I32 = mybir.dt.int32
ALU = mybir.AluOpType
ACT = mybir.ActivationFunctionType
AX = mybir.AxisListType

P = 128
HEADS = 8
DH = 64
PAIRS = HEADS // 2
EPS = 1e-5

HI, LO = 0, 1
PASSES = ((HI, HI), (HI, LO), (LO, HI))


def build(nc, x, ctx_in, g_xattn, g_ffn, wq, wk, wv, wo, bout, gate_w, w_gate, w_up, w_down,
          ws_gate, ws_up, ws_down, out):
    B, S, H = x.shape
    _, M, C = ctx_in.shape
    INNER = HEADS * DH
    KT = H // P
    CT = 2
    CP = C // CT
    QT = S // P
    MT = INNER // P
    T = B * QT
    SCALE = DH ** -0.5

    N = B * S
    E, _, D = w_gate.shape
    KD = D // P
    TOP = 2
    R = QT * P
    SHARED = N // R
    ROUTED = N * TOP // R + E - 1
    TILES = SHARED + ROUTED
    SLOT_STEPS = 2 + 2 * 4
    LAST_PAIR = TILES // 2 * 2 - 2
    CUTS = SHARED - 2
    RW = H + 2
    IDC, WC = H, H + 1
    GW = 2 * KT * D
    RAW = GW + KD * H
    EARLY = 6

    xg = nc.dram_tensor("xg", (ROUTED * R, RW), F32, kind="Internal").ap()

    es = ExitStack()
    early = ExitStack()
    with es:
        def sb(name, shape, dt=F32):
            return es.enter_context(nc.sbuf_tensor(name, shape, dt))

        def sb_attn(name, shape, dt=F32):
            return early.enter_context(nc.sbuf_tensor(name, shape, dt))

        def sem(name):
            return es.enter_context(nc.semaphore(name))

        psum = es.enter_context(nc.psum_tensor("psum", [P, 8, 512], F32))
        SCORES = [psum[:, 0:2], psum[:, 2:4]]
        TURNED = [psum[:, 6:8], psum[:, 4:6]]
        BA0, BA1, BB0, BB1, BC0, BC1, BD, BE = (psum[:, n] for n in range(8))

        GATE, UP = [psum[:, 0], psum[:, 2]], [psum[:, 1], psum[:, 3]]
        YB, TXB = [psum[:, 4, 0:H], psum[:, 5, 0:H]], psum[:, 6]

        ident = sb("ident", [P, P])
        half = sb("half", [P, QT])
        gx = sb("gx", [P, 2])
        tg = sb("tg", [P, 2])
        xr = [sb(f"xr{k}", [P, T, RW]) for k in range(TOP)]
        xn2 = sb("xn2", [P, QT, H])
        x2T = sb("x2T", [P, 2, KT, S], F32R)
        gw_raw = sb("gw_raw", [P, KT, E])
        gw_s = sb("gw_s", [P, 2, KT, E], F32R)
        stats2 = sb("stats2", [P, QT, 6])
        mv2 = sb("mv2", [P, QT, 2])
        vare2 = sb("vare2", [P, QT])
        rstd2 = sb("rstd2", [P, QT])
        logit = sb("logit", [P, T, E])
        ones = sb("ones", [P, P])
        before = sb("before", [P, P])
        first = sb("first", [P, E])
        more = sb("more", [P, E, E])
        count_i = sb("count_i", [P, ROUTED], I32)
        count = sb("count", [P, ROUTED])
        count_r = sb("count_r", [P, E])
        etab = sb("etab", [1, ROUTED + 2], I32)
        pos = sb("pos", [P, TOP, T], U32)
        pad = sb("pad", [P, QT, RW])

        crow = sb_attn("crow", [M, B, C])
        cbuf = sb_attn("cbuf", [M, C])
        wq_s = sb_attn("wq_s", [P, 2, KT, INNER], F32R)
        wk_s = sb_attn("wk_s", [CP, 2, CT, INNER], F32R)
        wv_s = sb_attn("wv_s", [CP, 2, CT, INNER], F32R)
        bias = sb_attn("bias", [P, H])

        stats = sb_attn("stats", [P, QT, 6])
        mv = sb_attn("mv", [P, QT, 2])
        vare = sb_attn("vare", [P, QT])
        rstd = sb_attn("rstd", [P, QT])
        xn = sb_attn("xn", [P, QT, H])
        xT = sb_attn("xT", [P, 2, KT, S], F32R)
        cT = sb_attn("cT", [CP, 2, CT, M], F32R)
        qT = sb_attn("qT", [P, 2, MT, S], F32R)
        kz = sb_attn("kz", [P, 2, PAIRS, 2, M], F32R)
        vz = sb_attn("vz", [M, 2, HEADS, P], F32R)
        prob = sb_attn("prob", [P, QT, HEADS, M])
        mx = sb_attn("mx", [P, QT, HEADS])
        den = sb_attn("den", [P, QT, HEADS])
        rden = sb_attn("rden", [P, QT, HEADS])
        pT = sb_attn("pT", [M, 2, HEADS, S], F32R)
        oT = sb_attn("oT", [P, 2, PAIRS, S], F32R)
        wo_s = sb_attn("wo_s", [P, 2, MT, H], F32R)
        rows = sb_attn("rows", [P, T, H])
        wstage = xr[0][:].rearrange("p t c -> p (t c)")[:, 0:4 * 1024].rearrange("p (n c) -> p n c", n=4)
        early.close()

        wgu = [sb(f"wgu{h}", [P, 2, 2 * KT, D // 2], F32R) for h in range(2)]
        wdn = [sb(f"wdn{h}", [P, 2, KD // 2, H], F32R) for h in range(2)]
        xin = sb("xin", [P, 2, QT, RW])
        tx = [sb(f"tx{n}", [P, 2, KT, R], F32R) for n in range(2)]
        meta = sb("meta", [P, 2, QT, 2])
        hid = sb("hid", [P, 2, 2 * R])
        hs = [sb(f"hs{h}", [P, 2, KD // 2, R], F32R) for h in range(2)]
        ys = sb("ys", [P, 2, QT, H])

        small = [sb_attn(f"small{n}", [P, T]) for n in range(7)]
        slot_f = [sb_attn(f"slot_f{k}", [P, T]) for k in range(TOP)]
        score = sb_attn("score", [P, T, E])
        shift = sb_attn("shift", [P, T, E])
        sel = [sb_attn(f"sel{k}", [P, T, E]) for k in range(TOP)]
        mask = sb_attn("mask", [P, T, E])
        inside = sb_attn("inside", [P, T, E])
        total = sb_attn("total", [P, T, E])
        cum = [sb_attn(f"cum{n}", [P, T, E]) for n in range(2)]
        slot = sb_attn("slot", [P, T, E])
        picked = [sb_attn(f"picked{k}", [P, T, E]) for k in range(TOP)]
        tokens_e = sb_attn("tokens_e", [P, E])
        square = sb_attn("square", [P, E, E])
        square2 = sb_attn("square2", [P, E, E])
        tiles_e = sb_attn("tiles_e", [P, E])
        base_e = sb_attn("base_e", [P, E])
        owner = sb_attn("owner", [1, ROUTED, E])
        owner_f = sb_attn("owner_f", [1, ROUTED])
        equal = sb_attn("equal", [P, T, E])
        rest = sb_attn("rest", [P, T, E])
        early.close()
        raw = sb("raw", [P, E + 1, RAW])

        s_x = sem("s_x")
        s_c = sem("s_c")
        s_g = sem("s_g")
        s_b = sem("s_b")
        s_w = [sem(f"s_w{n}") for n in range(4)]
        ident_ready = sem("ident_ready")
        const_ready = sem("const_ready")
        zero_ready = sem("zero_ready")
        tanh_ready = sem("tanh_ready")
        bias_ready = sem("bias_ready")
        whi_ready = sem("whi_ready")
        wlo_ready = sem("wlo_ready")
        stat_step = sem("stat_step")
        stat_ready = sem("stat_ready")
        stat_passed = sem("stat_passed")
        var_passed = sem("var_passed")
        rstd_step = sem("rstd_step")
        rstd_ready = sem("rstd_ready")
        xn_ready = sem("xn_ready")
        ctx_ready = sem("ctx_ready")
        biased = sem("biased")
        xT_done, xT_hi, xT_lo = sem("xT_done"), sem("xT_hi"), sem("xT_lo")
        cT_done, cT_hi, cT_lo = sem("cT_done"), sem("cT_hi"), sem("cT_lo")
        q_done, q_hi, q_lo = sem("q_done"), sem("q_hi"), sem("q_lo")
        k_done, k_hi, k_lo = sem("k_done"), sem("k_hi"), sem("k_lo")
        v_done, v_hi, v_lo = sem("v_done"), sem("v_hi"), sem("v_lo")
        s_done = sem("s_done")
        max_ready, sub_ready, exp_ready = sem("max_ready"), sem("sub_ready"), sem("exp_ready")
        den_ready, rden_ready, norm_ready = sem("den_ready"), sem("rden_ready"), sem("norm_ready")
        p_done, p_hi, p_lo = sem("p_done"), sem("p_hi"), sem("p_lo")
        o_done, o_hi, o_lo = sem("o_done"), sem("o_hi"), sem("o_lo")
        y_done, y_added = sem("y_done"), sem("y_added")
        s_rows = sem("s_rows")
        s_x0 = sem("s_x0")
        sp_passed = sem("sp_passed")
        s_res = [sem(f"s_res{n}") for n in range(2)]
        s_stored = [sem(f"s_stored{n}") for n in range(2)]
        s_pad = sem("s_pad")
        s_zero = sem("s_zero")
        s_raw = [sem(f"s_raw{e}") for e in range(E + 1)]
        s_slots = sem("s_slots")
        x_loaded = [sem(f"x_loaded{n}") for n in range(2)]
        s_added = sem("s_added")
        pad_ready, id_ready = sem("pad_ready"), sem("id_ready")
        s_gw, gw_hi, gw_lo = sem("s_gw"), sem("gw_hi"), sem("gw_lo")
        stat2_step, stat2_ready, stat2_passed = sem("stat2_step"), sem("stat2_ready"), sem("stat2_passed")
        var2_passed, rstd2_step, rstd2_ready = sem("var2_passed"), sem("rstd2_step"), sem("rstd2_ready")
        xn2_ready, row0_ready, row1_ready = sem("xn2_ready"), sem("row0_ready"), sem("row1_ready")
        x2_done, x2_hi, x2_lo = sem("x2_done"), sem("x2_hi"), sem("x2_lo")
        l_done, l_ready = sem("l_done"), sem("l_ready")
        route_step = sem("route_step")
        shifted, expd = sem("shifted"), sem("expd")
        mask_ready, prefix_done = sem("mask_ready"), sem("prefix_done")
        counts_ready, slot_step = sem("counts_ready"), sem("slot_step")
        sum_ready, weight_ready = sem("sum_ready"), sem("weight_ready")
        pos_ready, etab_ready = sem("pos_ready"), sem("etab_ready")
        tx_done, tx_hi, tx_lo = sem("tx_done"), sem("tx_hi"), sem("tx_lo")
        gu_done, silu_ready, h_ready = sem("gu_done"), sem("silu_ready"), sem("h_ready")
        h_hi, h_lo = sem("h_hi"), sem("h_lo")
        d_done, y_ready = sem("d_done"), sem("y_ready")
        w_hi = [sem(f"w_hi{g}") for g in range(4)]
        w_lo = [sem(f"w_lo{g}") for g in range(4)]
        meta_ready, pool_passed = sem("meta_ready"), sem("pool_passed")

        def f32(ap):
            return ap.bitcast(F32)

        def flat(ap):
            return ap.rearrange("p a b -> p (a b)")

        def group_raw(e, g):
            w = raw[:, bass.ds(e, 1)].squeeze(1)
            if g < 2:
                return w[:, 0:GW].rearrange("p (a n) -> p a n", n=D)[:, :, g * (D // 2):(g + 1) * (D // 2)]
            n = KD // 2 * H
            return w[:, GW + (g - 2) * n:GW + (g - 1) * n].rearrange("p (a n) -> p a n", n=H)

        def group_split(g, part):
            return (wgu[g] if g < 2 else wdn[g - 2])[:, part]

        def expert(eng, t):
            return eng.value_load(etab[0:1, bass.ds(t - SHARED, 1)], min_val=0, max_val=E - 1)

        def over_tiles(eng, step, routed_from_here=None):
            def peeled(t):
                step(t, t % 2, lambda d: t + d >= SHARED)

            peeled(0)
            peeled(1)
            with eng.Fori(1, SHARED // 2 - 1) as u:
                for p in range(2):
                    step(u * 2 + p, p, lambda d: False)
            if routed_from_here:
                routed_from_here()
            peeled(SHARED - 2)
            peeled(SHARED - 1)
            over_routed(eng, step)

        def over_routed(eng, step):
            with eng.Fori(SHARED // 2, LAST_PAIR // 2) as u:
                for p in range(2):
                    step(u * 2 + p, p, lambda d: True)
            for t in range(LAST_PAIR, TILES):
                step(t, t % 2, lambda d: True)

        def cuts(t, routed):
            return t - CUTS if routed else 1

        def has(n):
            return not isinstance(n, int) or 0 <= n < B

        def is_last(b):
            return isinstance(b, int) and b == B

        def over_batches(eng, step, before_last=None):
            step(0)
            step(1)
            with eng.Fori(2, B - 2) as b:
                step(b)
            for b in range(B - 2, B + 1):
                if b == B and before_last:
                    before_last()
                step(b)

        def exists(t):
            return not isinstance(t, int) or t < TILES

        block = es.enter_context(nc.Block())

        @block.sync
        def _(sp):
            def load_expert(sp, e):
                gate, up, down = (w_gate[e], w_up[e], w_down[e]) if e < E else (ws_gate, ws_up, ws_down)
                for n, w in enumerate((gate, up)):
                    sp.dma_start(raw[:, e, n * KT * D:(n + 1) * KT * D].rearrange("p (k d) -> p k d", d=D),
                                 w.rearrange("(k p) d -> p k d", p=P)).then_inc(s_raw[e], 16)
                sp.dma_start(raw[:, e, GW:RAW].rearrange("p (m h) -> p m h", h=H),
                             down.rearrange("(m p) h -> p m h", p=P)).then_inc(s_raw[e], 16)

            x_rows = x.rearrange("b (j p) h -> p (b j) h", p=P)
            sp.dma_start(rows[:, 0:QT], x_rows[:, 0:QT]).then_inc(s_x0, 16)

            def load_matrix(n, w, k):
                part = w.shape[0] // k
                sp.dma_start(wstage[0:part, n].rearrange("p (k n) -> p k n", k=k),
                             w.rearrange("(k p) n -> p k n", k=k)).then_inc(s_w[n], 16)

            load_matrix(0, wq, KT)
            sp.dma_start(crow[:], ctx_in.rearrange("b m c -> m b c")).then_inc(s_c, 16)
            load_matrix(1, wk, CT)
            sp.dma_start(rows[:, QT:T], x_rows[:, QT:T]).then_inc(s_x, 16)
            load_matrix(2, wv, CT)
            load_matrix(3, wo, MT)
            sp.dma_start(gw_raw[:], gate_w.rearrange("(k p) e -> p k e", p=P)).then_inc(s_gw, 16)
            for e in range(E, EARLY - 1, -1):
                load_expert(sp, e)
            sp.wait_ge(pad_ready, 2)
            with sp.Fori(0, ROUTED) as t:
                sp.dma_start(xg[bass.ds(t * R, R)].rearrange("(j p) c -> p j c", p=P), pad[:]).then_inc(s_pad, 16)
            sp.dma_start(out[N:N + R].rearrange("(j p) h -> p j h", p=P), pad[:, :, 0:H]).then_inc(s_zero, 16)

            def store_rows(b):
                sp.wait_ge(y_added, b + 1)
                sp.dma_start(out[bass.ds(b * S, S)].rearrange("(j p) h -> p j h", p=P),
                             rows[:, bass.ds(b * QT, QT)]).then_inc(s_rows, 16)

            def shared_rows(t):
                sp.dma_start(xin[:, t % 2, :, 0:H], xr[0][:, t * QT:(t + 1) * QT, 0:H]).then_inc(x_loaded[t % 2], 16)

            def residual(t):
                sp.dma_start(ys[:, t % 2], out[t * R:(t + 1) * R].rearrange("(j q) h -> q j h", q=P)) \
                    .then_inc(s_res[t % 2], 16)

            def slot_rows(start, p):
                sp.dma_start(xin[:, p], xg[bass.ds(start, R)].rearrange("(j q) c -> q j c", q=P)) \
                    .then_inc(x_loaded[p], 16)

            with sp.Fori(0, B - 1) as b:
                store_rows(b)
            sp.wait_ge(k_done, B)
            for t in range(2):
                sp.wait_ge(row0_ready, t + 1)
                shared_rows(t)
            store_rows(B - 1)
            sp.wait_ge(s_rows, 16 * B)
            residual(0)
            sp.wait_ge(row0_ready, B)
            later = {0: (5, 4), 1: (3,), 2: (2,), 3: (1,), 4: (0,)}
            for t in range(SHARED):
                sp.wait_ge(tx_done, t + 1)
                if t + 2 < SHARED:
                    shared_rows(t + 2)
                if t + 1 < SHARED:
                    if t >= 1:
                        sp.wait_ge(s_stored[(t + 1) % 2], 16 * ((t + 1) // 2))
                    residual(t + 1)
                for e in later.get(t, ()):
                    if e == 1:
                        sp.wait_ge(etab_ready, 1)
                        sp.wait_ge(weight_ready, 3)
                    load_expert(sp, e)
                if t == SHARED - 2:
                    sp.wait_ge(s_slots, 16 * TOP * T)
                    slot_rows(0, 0)
                    sp.wait_ge(tx_done, SHARED)
                    slot_rows(R, 1)
                sp.wait_ge(y_ready, t + 1)
                sp.dma_start(out[t * R:(t + 1) * R].rearrange("(j q) h -> q j h", q=P), ys[:, t % 2]) \
                    .then_inc(s_stored[t % 2], 16)

            def refill(t, p, routed):
                if exists(t + 2):
                    start = t * R + (2 * R - N)
                    if not isinstance(t, int):
                        start = sp.snap(start)
                    sp.wait_ge(tx_done, t + 1)
                    sp.sem_inc(sp_passed, 1)
                    sp.wait_ge(meta_ready, t - (SHARED - 1))
                    slot_rows(start, p)

            over_routed(sp, refill)
            sp.wait_ge(s_added, 16 * QT * ROUTED)

        @block.gpsimd
        def _(pool):
            nc.gpsimd.memset(ident[:], 0.0).then_inc(const_ready, 1)
            nc.gpsimd.memset(half[:], -0.5).then_inc(const_ready, 1)
            pool.wait_ge(const_ready, 2)
            nc.gpsimd.affine_select(out=ident[:], in_=ident[:], compare_op=ALU.not_equal, fill=1.0,
                                    base=0, pattern=[[-1, P]], channel_multiplier=1).then_inc(ident_ready, 1)
            pool.dma_start(gx[:, 0:1], g_xattn.partition_broadcast(P)).then_inc(s_g, 16)
            pool.dma_start(gx[:, 1:2], g_ffn.partition_broadcast(P)).then_inc(s_g, 16)
            pool.dma_start(bias[:], bout.partition_broadcast(P)).then_inc(s_b, 16)
            def context(n):
                pool.wait_ge(cT_done, n)
                nc.gpsimd.tensor_copy(cbuf[:], crow[:, bass.ds(n, 1)].squeeze(1)).then_inc(ctx_ready, 1)

            def prepare(n):
                pool.wait_ge(stat_ready, n + 1)
                pool.sem_inc(var_passed, 1)
                nc.gpsimd.tensor_scalar(vare[:], mv[:, :, 1], EPS, None, ALU.add).then_inc(rstd_step, 1)
                pool.wait_ge(rstd_step, n + 1)
                nc.gpsimd.tensor_tensor(rstd[:], vare[:], half[:], ALU.pow).then_inc(rstd_ready, 1)

            def prepare2(n):
                pool.wait_ge(stat2_ready, n + 1)
                pool.sem_inc(pool_passed, 1)
                nc.gpsimd.tensor_scalar(vare2[:], mv2[:, :, 1], EPS, None, ALU.add).then_inc(rstd2_step, 1)
                pool.wait_ge(rstd2_step, n + 1)
                nc.gpsimd.tensor_tensor(rstd2[:], vare2[:], half[:], ALU.pow).then_inc(rstd2_ready, 1)

            def keep_rows(n):
                pool.wait_ge(xn2_ready, n + 1)
                nc.gpsimd.tensor_copy(xr[1][:, bass.ds(n * QT, QT), 0:H], xn2[:]).then_inc(row1_ready, 1)

            def normalise(b, j):
                pool.wait_ge(rden_ready, QT * b + j + 1)
                nc.gpsimd.tensor_tensor(prob[:, j], prob[:, j], rden[:, j].unsqueeze(2).to_broadcast([P, HEADS, M]),
                                        ALU.mult).then_inc(norm_ready, 1)

            def add_bias(b):
                pool.wait_ge(xn_ready, b + 1)
                r = rows[:, bass.ds(b * QT, QT)]
                nc.gpsimd.tensor_tensor(r, r, bias[:].unsqueeze(1).to_broadcast([P, QT, H]),
                                        ALU.add).then_inc(biased, 1)

            def step(b):
                if has(b - 2):
                    prepare2(b - 2)
                if has(b + 1):
                    context(b + 1)
                if has(b):
                    normalise(b, 0)
                if has(b - 2):
                    keep_rows(b - 2)
                if has(b + 2):
                    prepare(b + 2)
                if has(b):
                    normalise(b, 1)
                    add_bias(b)

            prepare(0)
            nc.gpsimd.memset(f32(kz[:]), 0.0).then_inc(zero_ready, 1)
            pool.wait_ge(s_c, 16)
            context(0)
            nc.gpsimd.memset(f32(vz[:]), 0.0).then_inc(zero_ready, 1)
            nc.gpsimd.memset(pad[:], 0.0).then_inc(pad_ready, 1)
            pool.wait_ge(pad_ready, 1)
            nc.gpsimd.iota(pad[:, :, IDC].bitcast(I32), pattern=[[P, QT]], base=N, channel_multiplier=1) \
                .then_inc(pad_ready, 1)

            nc.gpsimd.memset(ones[:], 1.0).then_inc(const_ready, 1)
            for t in (more, before):
                nc.gpsimd.memset(t[:], 1.0).then_inc(const_ready, 1)
            nc.gpsimd.iota(count_i[:], pattern=[[1, ROUTED]], base=0, channel_multiplier=0).then_inc(const_ready, 1)
            pool.wait_ge(const_ready, 6)
            nc.gpsimd.affine_select(out=more[:], in_=more[:], compare_op=ALU.is_gt, fill=0.0, base=0,
                                    pattern=[[-1, E], [1, E]], channel_multiplier=0).then_inc(const_ready, 1)
            nc.gpsimd.affine_select(out=before[:], in_=before[:], compare_op=ALU.is_gt, fill=0.0, base=0,
                                    pattern=[[1, P]], channel_multiplier=-1).then_inc(const_ready, 1)

            prepare(1)
            pool.wait_ge(s_b, 16)
            pool.wait_ge(tanh_ready, 1)
            nc.gpsimd.tensor_scalar(bias[:], bias[:], tg[:, 0:1], None, ALU.mult).then_inc(bias_ready, 1)
            pool.wait_ge(bias_ready, 1)
            over_batches(pool, step)

            split_low_shared = [group_raw(E, g) for g in range(4)]
            for g in (1, 2):
                pool.wait_ge(w_hi[g], 1)
                nc.gpsimd.tensor_tensor(group_split(g, LO), split_low_shared[g], f32(group_split(g, HI)),
                                        ALU.subtract).then_inc(w_lo[g], 1)

            pool.wait_ge(wlo_ready, 4)
            for k in range(TOP):
                nc.gpsimd.iota(xr[k][:, :, IDC].bitcast(I32), pattern=[[P, T]], base=0, channel_multiplier=1) \
                    .then_inc(id_ready, 1)
            prepare2(B - 1)
            keep_rows(B - 1)

            slot_steps = 0
            src = total
            pool.wait_ge(counts_ready, 1)
            for n, d in enumerate((1, 2, 4, 8)):
                dst = cum[n % 2]
                nc.gpsimd.tensor_copy(dst[:, 0:d], src[:, 0:d]).then_inc(slot_step, 1)
                nc.gpsimd.tensor_tensor(dst[:, d:T], src[:, d:T], src[:, 0:T - d], ALU.add).then_inc(slot_step, 1)
                slot_steps += 2
                pool.wait_ge(slot_step, slot_steps)
                src = dst
            nc.gpsimd.tensor_tensor(slot[:], src[:], total[:], ALU.subtract).then_inc(slot_step, 1)
            pool.wait_ge(slot_step, slot_steps + 1)
            nc.gpsimd.tensor_tensor(slot[:], slot[:], inside[:], ALU.add).then_inc(slot_step, 1)

            top1, top2, part, scale = (small[n][:] for n in (0, 1, 4, 6))
            pool.wait_ge(sum_ready, 1)
            nc.gpsimd.tensor_scalar(scale, part, tg[:, 1:2], None, ALU.mult).then_inc(weight_ready, 1)
            pool.wait_ge(weight_ready, 1)
            nc.gpsimd.tensor_tensor(xr[0][:, :, WC], top1, scale, ALU.mult).then_inc(weight_ready, 1)
            nc.gpsimd.tensor_tensor(xr[1][:, :, WC], top2, scale, ALU.mult).then_inc(weight_ready, 1)

            pool.wait_ge(weight_ready, 3)
            pool.wait_ge(id_ready, TOP)
            pool.wait_ge(row0_ready, B)
            pool.wait_ge(row1_ready, B)
            pool.wait_ge(pos_ready, 1)
            pool.wait_ge(s_pad, 16 * ROUTED)
            for j in range(T):
                for k in range(TOP):
                    pool.indirect_dma_start(out=xg, out_offset=bass.IndirectOffsetOnAxis(ap=pos[:, k, j:j + 1], axis=0),
                                            in_=xr[k][:, j, :], in_offset=None).then_inc(s_slots, 16)

            def split_low(number, g, e):
                pool.wait_ge(w_hi[g], number)
                nc.gpsimd.tensor_tensor(group_split(g, LO), group_raw(e, g), f32(group_split(g, HI)),
                                        ALU.subtract).then_inc(w_lo[g], 1)

            def copy_meta(t, p):
                pool.wait_ge(x_loaded[p], (t // 2 + 1) * 16 if isinstance(t, int) else t * 8 + (16 - 8 * p))
                pool.sem_inc(pool_passed, 1)
                nc.gpsimd.tensor_copy(meta[:, p], xin[:, p, :, IDC:RW]).then_inc(meta_ready, 1)

            def tile(t, p, routed):
                if exists(t + 1):
                    e1 = expert(pool, t + 1)
                    split_low(cuts(t + 1, True), 1, e1)
                    split_low(cuts(t + 1, True), 2, e1)
                if isinstance(t, int) or routed(-1):
                    pool.wait_ge(s_added, t * (16 * QT) - 16 * QT * SHARED)
                    pool.sem_inc(pool_passed, 1)
                if exists(t + 1):
                    copy_meta(t + 1, 1 - p)
                pool.wait_ge(y_ready, t + 1)
                pool.sem_inc(pool_passed, 1)
                for j in range(QT):
                    pool.indirect_dma_start(
                        out=out, out_offset=bass.IndirectOffsetOnAxis(ap=meta[:, p, j, 0:1].bitcast(U32), axis=0),
                        in_=ys[:, p, j], in_offset=None, compute_op=ALU.add).then_inc(s_added, 16)

            pool.wait_ge(etab_ready, 1)
            for e in range(E):
                pool.wait_ge(s_raw[e], 48)
            e0 = expert(pool, SHARED)
            copy_meta(SHARED, 0)
            split_low(2, 1, e0)
            split_low(2, 2, e0)
            pool.wait_ge(s_zero, 16)
            for n in range(2):
                pool.wait_ge(s_stored[n], 16 * (SHARED // 2))
            tile(SHARED, 0, lambda d: d >= 0)
            tile(SHARED + 1, 1, lambda d: True)
            with pool.Fori(SHARED // 2 + 1, LAST_PAIR // 2) as u:
                for p in range(2):
                    tile(u * 2 + p, p, lambda d: True)
            for t in range(LAST_PAIR, TILES):
                tile(t, t % 2, lambda d: True)

        @block.scalar
        def _(act):
            def matrix_high(n):
                w, part = ((wq_s, P), (wk_s, CP), (wv_s, CP), (wo_s, P))[n]
                act.wait_ge(s_w[n], 16)
                nc.scalar.copy(w[:, HI].rearrange("p k n -> p (k n)"), wstage[0:part, n]).then_inc(whi_ready, 1)

            def transposed(n):
                act.wait_ge(xT_done, n + 1)
                nc.scalar.copy(xT[:, HI].rearrange("p k s -> p (k s)"), BC1).then_inc(xT_hi, 1)

            def transposed_context(n):
                act.wait_ge(cT_done, n + 1)
                nc.scalar.copy(cT[:, HI].rearrange("p k s -> p (k s)"), BC1[0:CP, 0:CT * M]).then_inc(cT_hi, 1)

            def projected(n):
                for i, bank in enumerate((BA0, BA1)):
                    act.wait_ge(q_done, 2 * n + i + 1)
                    nc.scalar.mul(qT[:, HI, 2 * i:2 * i + 2].rearrange("p k s -> p (k s)"), bank, SCALE) \
                        .then_inc(q_hi, 1)

            def projected_keys(n):
                act.wait_ge(k_done, n + 1)
                act.wait_ge(zero_ready, 1)
                for a in range(2):
                    r = slice(a * DH, (a + 1) * DH)
                    i = nc.scalar.copy(kz[r, HI, :, a], BB0[r, 0:MT * M].rearrange("p (m k) -> p m k", k=M))
                i.then_inc(k_hi, 1)

            def exp(b, j):
                act.wait_ge(max_ready, QT * b + j + 1)
                sc = SCORES[j][:, :, 0:4 * M].rearrange("p c (h k) -> p c h k", k=M)
                for h in range(HEADS):
                    i = nc.scalar.activation(prob[:, j, h], sc[:, h // 4, h % 4], ACT.Exp, bias=mx[:, j, h:h + 1],
                                             accum_out=den[:, j, h:h + 1])
                i.then_inc(exp_ready, 1)

            def values(b):
                act.wait_ge(v_done, b + 1)
                act.wait_ge(zero_ready, 2)
                v = vz[:, HI].rearrange("p (g a) (c d) -> p g (a c) d", a=2, c=2)[:, :, 0:4:3]
                nc.scalar.copy(v, BE[0:M].rearrange("p (g a d) -> p g a d", g=PAIRS, a=2)).then_inc(v_hi, 1)

            def turned(b):
                for i in range(2):
                    act.wait_ge(p_done, 2 * b + i + 1)
                    nc.scalar.copy(pT[:, HI, 4 * i:4 * i + 4].rearrange("p (c h) s -> p c (h s)", c=2),
                                   TURNED[i][0:M]).then_inc(p_hi, 1)

            def attended(b, i):
                act.wait_ge(o_done, 2 * b + i + 1)
                nc.scalar.copy(oT[:, HI, 2 * i:2 * i + 2].rearrange("p k s -> p (k s)"), (BD, BC0)[i]).then_inc(o_hi, 1)

            def normed(n):
                act.wait_ge(xn2_ready, n + 1)
                nc.scalar.copy(xr[0][:, bass.ds(n * QT, QT), 0:H], xn2[:]).then_inc(row0_ready, 1)
                act.wait_ge(x2_done, n + 1)
                nc.scalar.copy(flat(x2T[:, HI]), BC0).then_inc(x2_hi, 1)

            def split_high(t, g, e):
                nc.scalar.copy(group_split(g, HI), group_raw(e, g)).then_inc(w_hi[g], 1)

            def rows_high(t, p):
                act.wait_ge(tx_done, t + 1)
                nc.scalar.copy(flat(tx[p][:, HI]), TXB).then_inc(tx_hi, 1)

            def step(b):
                if has(b - 1):
                    turned(b - 1)
                if has(b + 1):
                    transposed(b + 1)
                if has(b):
                    exp(b, 0)
                if has(b - 1):
                    attended(b - 1, 0)
                    attended(b - 1, 1)
                if is_last(b):
                    rows_high(0, 0)
                if has(b + 1):
                    transposed_context(b + 1)
                if has(b):
                    exp(b, 1)
                    values(b)
                if has(b + 1):
                    projected(b + 1)
                if has(b - 2):
                    normed(b - 2)
                if has(b + 1):
                    projected_keys(b + 1)

            def shared_high():
                act.wait_ge(s_raw[E], 48)
                for g in range(4):
                    split_high(0, g, E)

            matrix_high(0)
            transposed(0)
            matrix_high(1)
            transposed_context(0)
            act.wait_ge(s_g, 32)
            nc.scalar.activation(tg[:], gx[:], ACT.Tanh).then_inc(tanh_ready, 1)
            projected(0)
            matrix_high(2)
            projected_keys(0)
            matrix_high(3)
            act.wait_ge(s_gw, 16)
            nc.scalar.copy(gw_s[:, HI], gw_raw[:]).then_inc(gw_hi, 1)
            over_batches(act, step, shared_high)
            def silu(t, h):
                act.wait_ge(gu_done, t * 2 + h + 1)
                nc.scalar.activation(hid[:, h], GATE[h], ACT.Silu).then_inc(silu_ready, 1)

            def hidden_high(t, h):
                act.wait_ge(h_ready, t * 2 + h + 1)
                nc.scalar.copy(flat(hs[h][:, HI]), hid[:, h]).then_inc(h_hi, 1)

            silu(0, 0)
            hidden_high(0, 0)
            silu(0, 1)
            normed(B - 1)
            hidden_high(0, 1)


            def tile(t, p, routed):
                e1 = expert(act, t + 1) if exists(t + 1) and routed(1) else None
                e2 = expert(act, t + 2) if exists(t + 2) and routed(2) else None
                late = isinstance(t, int) and t == SHARED - 1
                if exists(t + 1) and not late:
                    rows_high(t + 1, 1 - p)
                begun = isinstance(t, int) and t == 0
                if begun:
                    act.wait_ge(shifted, 1)
                    nc.scalar.activation(score[:], shift[:], ACT.Exp).then_inc(expd, 1)
                else:
                    silu(t, 1)
                if isinstance(t, int) and t == 1:
                    act.wait_ge(prefix_done, 1)
                    nc.scalar.copy(flat(inside[:]), BE[:, 0:T * E])
                    nc.scalar.copy(flat(total[:]), BE[:, T * E:2 * T * E]).then_inc(counts_ready, 1)
                if e1 is not None:
                    split_high(t + 1, 1, e1)
                if not begun:
                    hidden_high(t, 1)
                if e1 is not None:
                    act.wait_ge(d_done, t * 2 + 1)
                    split_high(t + 1, 2, e1)
                if late:
                    rows_high(t + 1, 1 - p)
                if exists(t + 1):
                    silu(t + 1, 0)
                    if e2 is not None:
                        split_high(t + 2, 0, e2)
                    hidden_high(t + 1, 0)
                if e1 is not None:
                    act.wait_ge(d_done, t * 2 + 2)
                    split_high(t + 1, 3, e1)

            def all_weights():
                act.wait_ge(etab_ready, 1)
                for e in range(E):
                    act.wait_ge(s_raw[e], 48)

            over_tiles(act, tile, all_weights)

        @block.vector
        def _(dve):
            def low(dst, src, hi, done):
                nc.vector.tensor_tensor(dst, src, hi, ALU.subtract).then_inc(done, 1)

            def matrix_low(n):
                w, part = ((wq_s, P), (wk_s, CP), (wv_s, CP), (wo_s, P))[n]
                dve.wait_ge(whi_ready, n + 1)
                low(flat(w[:, LO]), wstage[0:part, n], flat(f32(w[:, HI])), wlo_ready)

            def statistics(n):
                for j in range(QT):
                    nc.vector.bn_stats(stats[:, j], rows[:, bass.ds(n * QT + j, 1)].squeeze(1)).then_inc(stat_step, 1)
                dve.wait_ge(stat_step, QT * n + QT)
                dve.sem_inc(stat_passed, 1)
                for j in range(QT):
                    i = nc.vector.bn_aggr(mv[:, j], stats[:, j])
                i.then_inc(stat_ready, 1)

            def layer_norm(n):
                dve.wait_ge(stat_ready, n + 1)
                dve.wait_ge(rstd_ready, n + 1)
                dve.wait_ge(xT_done, n)
                for j in range(QT):
                    i = nc.vector.tensor_scalar(xn[:, j], rows[:, bass.ds(n * QT + j, 1)].squeeze(1), mv[:, j, 0:1],
                                                rstd[:, j:j + 1], ALU.subtract, ALU.mult)
                i.then_inc(xn_ready, 1)

            def transposed(n):
                dve.wait_ge(xT_hi, n + 1)
                low(flat(xT[:, LO]), BC1, flat(f32(xT[:, HI])), xT_lo)

            def transposed_context(n):
                dve.wait_ge(cT_hi, n + 1)
                low(flat(cT[:, LO]), BC1[0:CP, 0:CT * M], flat(f32(cT[:, HI])), cT_lo)

            def projected(n):
                for i, bank in enumerate((BA0, BA1)):
                    dve.wait_ge(q_hi, 2 * n + i + 1)
                    part = slice(2 * i, 2 * i + 2)
                    nc.vector.scalar_tensor_tensor(
                        out=flat(qT[:, LO, part]), in0=bank, scalar=SCALE, in1=flat(f32(qT[:, HI, part])),
                        op0=ALU.mult, op1=ALU.subtract).then_inc(q_lo, 1)

            def projected_keys(n):
                dve.wait_ge(k_hi, n + 1)
                for a in range(2):
                    r = slice(a * DH, (a + 1) * DH)
                    i = nc.vector.tensor_tensor(kz[r, LO, :, a], BB0[r, 0:MT * M].rearrange("p (m k) -> p m k", k=M),
                                                f32(kz[r, HI, :, a]), ALU.subtract)
                i.then_inc(k_lo, 1)

            def maximum(b, j):
                dve.wait_ge(s_done, QT * b + j + 1)
                sc = SCORES[j][:, :, 0:4 * M].rearrange("p c (h k) -> p c h k", k=M)
                nc.vector.tensor_reduce(mx[:, j].rearrange("p (c h) -> p c h", c=2), sc, AX.X, ALU.max,
                                        negate=True).then_inc(max_ready, 1)

            def denominator(b, j):
                dve.wait_ge(exp_ready, QT * b + j + 1)
                nc.vector.reciprocal(rden[:, j], den[:, j]).then_inc(rden_ready, 1)

            def values(b):
                dve.wait_ge(v_hi, b + 1)
                v = [vz[:, w].rearrange("p (g a) (c d) -> p g (a c) d", a=2, c=2)[:, :, 0:4:3] for w in (HI, LO)]
                low(v[LO], BE[0:M].rearrange("p (g a d) -> p g a d", g=PAIRS, a=2), f32(v[HI]), v_lo)

            def turned(b):
                for i in range(2):
                    dve.wait_ge(p_hi, 2 * b + i + 1)
                    q = [pT[:, w, 4 * i:4 * i + 4].rearrange("p (c h) s -> p c (h s)", c=2) for w in (HI, LO)]
                    low(q[LO], TURNED[i][0:M], f32(q[HI]), p_lo)

            def attended(b):
                for i, bank in enumerate((BD, BC0)):
                    dve.wait_ge(o_hi, 2 * b + i + 1)
                    part = slice(2 * i, 2 * i + 2)
                    low(flat(oT[:, LO, part]), bank, flat(f32(oT[:, HI, part])), o_lo)

            def add(b):
                dve.wait_ge(y_done, b + 1)
                dve.wait_ge(biased, b + 1)
                r = flat(rows[:, bass.ds(b * QT, QT)])
                nc.vector.scalar_tensor_tensor(out=r, in0=BC1, scalar=tg[:, 0:1], in1=r, op0=ALU.mult,
                                               op1=ALU.add).then_inc(y_added, 1)

            def statistics2(n):
                dve.wait_ge(y_added, n + 1)
                dve.sem_inc(stat2_passed, 1)
                for j in range(QT):
                    nc.vector.bn_stats(stats2[:, j], rows[:, bass.ds(n * QT + j, 1)].squeeze(1)).then_inc(stat2_step, 1)
                dve.wait_ge(stat2_step, QT * n + QT)
                dve.sem_inc(stat2_passed, 1)
                for j in range(QT):
                    i = nc.vector.bn_aggr(mv2[:, j], stats2[:, j])
                i.then_inc(stat2_ready, 1)

            def layer_norm2(n):
                dve.wait_ge(stat2_ready, n + 1)
                dve.wait_ge(rstd2_ready, n + 1)
                for j in range(QT):
                    i = nc.vector.tensor_scalar(xn2[:, j], rows[:, bass.ds(n * QT + j, 1)].squeeze(1), mv2[:, j, 0:1],
                                                rstd2[:, j:j + 1], ALU.subtract, ALU.mult)
                i.then_inc(xn2_ready, 1)

            def normed(n):
                dve.wait_ge(x2_hi, n + 1)
                low(flat(x2T[:, LO]), BC0, flat(f32(x2T[:, HI])), x2_lo)

            def logits(n):
                dve.wait_ge(l_done, n + 1)
                nc.vector.tensor_copy(logit[:, bass.ds(n * QT, QT)], BC0[:, 0:QT * E].rearrange("p (j e) -> p j e", e=E)) \
                    .then_inc(l_ready, 1)

            def rows_low(t, p):
                dve.wait_ge(tx_hi, t + 1)
                low(flat(tx[p][:, LO]), TXB, flat(f32(tx[p][:, HI])), tx_lo)

            def split_low(number, g, e):
                dve.wait_ge(w_hi[g], number)
                low(group_split(g, LO), group_raw(e, g), f32(group_split(g, HI)), w_lo[g])

            def step(b):
                if has(b - 1):
                    turned(b - 1)
                if has(b):
                    maximum(b, 0)
                    maximum(b, 1)
                if has(b + 1):
                    transposed(b + 1)
                if has(b - 2):
                    layer_norm2(b - 2)
                if has(b):
                    denominator(b, 0)
                if has(b - 1):
                    attended(b - 1)
                if is_last(b):
                    rows_low(0, 0)
                if has(b + 1):
                    transposed_context(b + 1)
                if has(b + 2):
                    statistics(b + 2)
                if has(b):
                    denominator(b, 1)
                    values(b)
                if has(b + 1):
                    projected(b + 1)
                if has(b - 2):
                    normed(b - 2)
                if has(b + 1):
                    projected_keys(b + 1)
                if has(b + 2):
                    layer_norm(b + 2)
                if has(b - 1):
                    add(b - 1)
                    statistics2(b - 1)
                if has(b - 2):
                    logits(b - 2)

            def shared_low():
                split_low(1, 0, E)
                split_low(1, 3, E)

            dve.wait_ge(s_x0, 16)
            statistics(0)
            layer_norm(0)
            matrix_low(0)
            transposed(0)
            matrix_low(1)
            transposed_context(0)
            projected(0)
            dve.wait_ge(s_x, 16)
            statistics(1)
            matrix_low(2)
            projected_keys(0)
            layer_norm(1)
            matrix_low(3)
            dve.wait_ge(gw_hi, 1)
            low(gw_s[:, LO], gw_raw[:], f32(gw_s[:, HI]), gw_lo)
            dve.wait_ge(tanh_ready, 1)
            def hidden(t, h):
                dve.wait_ge(silu_ready, t * 2 + h + 1)
                nc.vector.tensor_tensor(hid[:, h], hid[:, h], UP[h], ALU.mult).then_inc(h_ready, 1)

            def hidden_low(t, h):
                dve.wait_ge(h_hi, t * 2 + h + 1)
                low(flat(hs[h][:, LO]), hid[:, h], flat(f32(hs[h][:, HI])), h_lo)

            over_batches(dve, step, shared_low)
            layer_norm2(B - 1)
            hidden(0, 0)
            hidden_low(0, 0)
            normed(B - 1)
            hidden(0, 1)
            hidden_low(0, 1)
            logits(B - 1)

            steps = [0]

            def then(i):
                steps[0] += 1
                i.then_inc(route_step, 1)
                dve.wait_ge(route_step, steps[0])

            V = nc.vector
            s0, s1, s2, s3, s4, s5, _ = (t[:] for t in small)

            def over_e(ap):
                return ap.unsqueeze(2).to_broadcast([P, T, E])

            dve.wait_ge(l_ready, B)
            then(V.tensor_reduce(s0, logit[:], AX.X, ALU.max))
            V.tensor_tensor(shift[:], logit[:], over_e(s0), ALU.subtract).then_inc(shifted, 1)

            def best(k, src, top):
                then(V.tensor_reduce(top, src[:], AX.X, ALU.max))
                then(V.tensor_tensor(equal[:], src[:], over_e(top), ALU.is_equal))
                then(V.tensor_tensor(equal[:], equal[:], first[:].unsqueeze(1).to_broadcast([P, T, E]), ALU.mult))
                then(V.tensor_reduce(s5, equal[:], AX.X, ALU.max))
                then(V.tensor_tensor(sel[k][:], equal[:], over_e(s5), ALU.is_equal))

            def softmax_and_first_choice():
                dve.wait_ge(const_ready, 8)
                V.tensor_copy(count[:], count_i[:])
                dve.wait_ge(expd, 1)
                then(V.tensor_reduce(s1, score[:], AX.X, ALU.add))
                then(V.reciprocal(s2, s1))
                then(V.tensor_tensor(score[:], score[:], over_e(s2), ALU.mult))
                then(V.tensor_scalar(first[:], count[:, 0:E], -1.0, float(E), ALU.mult, ALU.add))
                V.tensor_scalar(count_r[:], count[:, 0:E], float(R), None, ALU.mult)

                best(0, score, s0)

            def second_choice():
                then(V.scalar_tensor_tensor(out=rest[:], in0=sel[0][:], scalar=-2.0, in1=score[:], op0=ALU.mult,
                                            op1=ALU.add))
                best(1, rest, s1)
                V.tensor_tensor(mask[:], sel[0][:], sel[1][:], ALU.add).then_inc(mask_ready, 1)
                then(V.tensor_tensor(s2, s0, s1, ALU.add))
                then(V.tensor_scalar(s3, s2, 1e-20, None, ALU.add))
                V.reciprocal(s4, s3).then_inc(sum_ready, 1)

            def bases_and_slots():
                dve.wait_ge(counts_ready, 1)
                then(V.tensor_reduce(tokens_e[:], total[:].rearrange("p t e -> p e t"), AX.X, ALU.add))
                then(V.tensor_tensor(square[:], tokens_e[:].unsqueeze(2).to_broadcast([P, E, E]),
                                     count_r[:].unsqueeze(1).to_broadcast([P, E, E]), ALU.is_gt))
                then(V.tensor_reduce(tiles_e[:], square[:], AX.X, ALU.add))
                then(V.tensor_tensor(square2[:], more[:], tiles_e[:].unsqueeze(1).to_broadcast([P, E, E]), ALU.mult))
                then(V.tensor_reduce(base_e[:], square2[:], AX.X, ALU.add))
                then(V.tensor_scalar(tiles_e[:], base_e[:], float(R), None, ALU.mult))

                dve.wait_ge(slot_step, SLOT_STEPS)
                then(V.tensor_tensor(slot[:], slot[:], tiles_e[:].unsqueeze(1).to_broadcast([P, T, E]), ALU.add))
                for k in range(TOP):
                    i = V.tensor_tensor(picked[k][:], sel[k][:], slot[:], ALU.mult)
                then(i)
                for k in range(TOP):
                    i = V.tensor_reduce(slot_f[k][:], picked[k][:], AX.X, ALU.add)
                then(i)
                for k in range(TOP):
                    i = V.tensor_copy(pos[:, k], slot_f[k][:])
                i.then_inc(pos_ready, 1)

            def owners():
                then(V.tensor_tensor(owner[:], base_e[0:1].unsqueeze(1).to_broadcast([1, ROUTED, E]),
                                     count[0:1].unsqueeze(2).to_broadcast([1, ROUTED, E]), ALU.is_gt))
                then(V.tensor_reduce(owner_f[:], owner[:], AX.X, ALU.add))
                V.tensor_copy(etab[0:1, 0:ROUTED], owner_f[:]).then_inc(etab_ready, 1)

            pieces = (softmax_and_first_choice, second_choice, bases_and_slots, owners)

            def weigh_shared(t):
                dve.wait_ge(d_done, t * 2 + 2)
                dve.wait_ge(s_res[t % 2], 16 * (t // 2 + 1))
                for j in range(QT):
                    i = V.scalar_tensor_tensor(out=ys[:, t % 2, j], in0=YB[j], scalar=tg[:, 1:2], in1=ys[:, t % 2, j],
                                               op0=ALU.mult, op1=ALU.add)
                i.then_inc(y_ready, 1)

            def weigh(t, p, routed):
                dve.wait_ge(d_done, t * 2 + 2)
                dve.wait_ge(meta_ready, t - (SHARED - 1))
                if isinstance(t, int) and t - 2 < SHARED:
                    dve.wait_ge(s_stored[p], 16 * (SHARED // 2))
                else:
                    dve.wait_ge(s_added, t * (16 * QT) - 16 * QT * (SHARED + 1))
                for j in range(QT):
                    i = V.tensor_scalar(ys[:, p, j], YB[j], meta[:, p, j, 1:2], None, ALU.mult)
                i.then_inc(y_ready, 1)

            def tile(t, p, routed, between=None):
                e0 = expert(dve, t) if routed(0) else None
                e2 = expert(dve, t + 2) if exists(t + 2) and routed(2) else None
                late = isinstance(t, int) and t == SHARED - 1
                if exists(t + 1) and not late:
                    rows_low(t + 1, 1 - p)
                if e0 is not None:
                    split_low(cuts(t, True), 3, e0)
                if not isinstance(t, int) or t > 0:
                    hidden(t, 1)
                    hidden_low(t, 1)
                if between:
                    between()
                if late:
                    rows_low(t + 1, 1 - p)
                if exists(t + 1):
                    hidden(t + 1, 0)
                if e0 is not None:
                    weigh(t, p, routed)
                else:
                    weigh_shared(t)
                if exists(t + 1):
                    hidden_low(t + 1, 0)
                if e2 is not None:
                    split_low(cuts(t + 2, True), 0, e2)

            for t in range(SHARED):
                tile(t, t % 2, lambda d: t + d >= SHARED, pieces[2 * t] if 2 * t < len(pieces) else None)
                if 2 * t + 1 < len(pieces):
                    pieces[2 * t + 1]()
                if t == SHARED - 3:
                    dve.wait_ge(etab_ready, 1)
                    for e in range(E):
                        dve.wait_ge(s_raw[e], 48)
            tile(SHARED, 0, lambda d: d >= 0)
            tile(SHARED + 1, 1, lambda d: True)
            with dve.Fori(SHARED // 2 + 1, LAST_PAIR // 2) as u:
                for p in range(2):
                    tile(u * 2 + p, p, lambda d: True)
            for t in range(LAST_PAIR, TILES):
                tile(t, t % 2, lambda d: True)

        @block.tensor
        def _(pe):
            pe.wait_ge(ident_ready, 1)

            def transposes(n):
                pe.wait_ge(xn_ready, n + 1)
                if has(n - 2):
                    pe.wait_ge(p_lo, 2 * n - 2)
                for k in range(KT):
                    for j in range(QT):
                        i = nc.tensor.transpose(BC1[:, k * S + j * P:k * S + j * P + P], xn[:, j, k * P:(k + 1) * P],
                                                ident[:])
                i.then_inc(xT_done, 1)

            def context_transposes(n):
                pe.wait_ge(ctx_ready, n + 1)
                pe.wait_ge(xT_lo, n + 1)
                for k in range(CT):
                    i = nc.tensor.transpose(BC1[0:CP, k * M:(k + 1) * M], cbuf[:, k * CP:(k + 1) * CP],
                                            ident[0:M, 0:M])
                i.then_inc(cT_done, 1)

            def product(dst, lhs, rhs, ks):
                for n, k in enumerate(ks):
                    for u, (a, c) in enumerate(PASSES):
                        i = nc.tensor.matmul(dst, lhs(a, k), rhs(c, k), start=(n == 0 and u == 0),
                                             stop=(n == len(ks) - 1 and u == 2))
                return i

            def projections(n):
                pe.wait_ge(xT_lo, n + 1)
                if has(n - 1):
                    pe.wait_ge(exp_ready, QT * n - 1)
                pe.wait_ge(wlo_ready, 1)
                for h, bank in enumerate((BA0, BA1)):
                    for m in range(2):
                        mt = 2 * h + m
                        i = product(bank[:, m * S:(m + 1) * S], lambda a, k: wq_s[:, a, k, mt * P:(mt + 1) * P],
                                    lambda a, k: xT[:, a, k], range(KT))
                    i.then_inc(q_done, 1)

            def projected_keys(n):
                pe.wait_ge(cT_lo, n + 1)
                pe.wait_ge(wlo_ready, 2)
                if has(n - 1):
                    pe.wait_ge(exp_ready, QT * n)
                for m in range(MT):
                    i = product(BB0[:, m * M:(m + 1) * M], lambda a, k: wk_s[:, a, k, m * P:(m + 1) * P],
                                lambda a, k: cT[:, a, k], range(CT))
                i.then_inc(k_done, 1)

            def scores(b):
                pe.wait_ge(q_lo, 2 * b + 2)
                pe.wait_ge(k_lo, b + 1)
                for j in range(QT):
                    for m in range(PAIRS):
                        i = product(SCORES[j][:, m // 2, (m % 2) * 2 * M:(m % 2 + 1) * 2 * M],
                                    lambda a, k: qT[:, a, m, j * P:(j + 1) * P],
                                    lambda a, k: kz[:, a, m].rearrange("p a k -> p (a k)"), (0,))
                    i.then_inc(s_done, 1)

            def values(b):
                if has(b - 1):
                    pe.wait_ge(p_lo, 2 * b)
                pe.wait_ge(wlo_ready, 3)
                product(BE[0:M], lambda a, k: cT[:, a, k], lambda a, k: wv_s[:, a, k], range(CT)) \
                    .then_inc(v_done, 1)

            def turn(b):
                pe.wait_ge(norm_ready, QT * b + QT)
                pe.wait_ge(v_lo, b + 1)
                for i in range(2):
                    if i == 1 and has(b - 1):
                        pe.wait_ge(y_added, b)
                    if i == 1 and has(b - 2):
                        pe.wait_ge(l_ready, b - 1)
                    for hh in range(4):
                        h = 4 * i + hh
                        for j in range(QT):
                            t = nc.tensor.transpose(TURNED[i][0:M, hh // 2, (hh % 2) * S + j * P:(hh % 2) * S + j * P + P],
                                                    prob[:, j, h], ident[:])
                    t.then_inc(p_done, 1)

            def attend(b):
                for i, bank in enumerate((BD, BC0)):
                    pe.wait_ge(p_lo, 2 * b + i + 1)
                    for g in range(2):
                        h = 4 * i + 2 * g
                        t = product(bank[:, g * S:(g + 1) * S], lambda a, k: vz[:, a, k],
                                    lambda a, k: pT[:, a, k], (h, h + 1))
                    t.then_inc(o_done, 1)

            def project_out(b):
                pe.wait_ge(o_lo, 2 * b + 2)
                pe.wait_ge(wlo_ready, 4)
                for j in range(QT):
                    t = product(BC1[:, j * H:(j + 1) * H], lambda a, k: oT[:, a, k, j * P:(j + 1) * P],
                                lambda a, k: wo_s[:, a, k], range(MT))
                t.then_inc(y_done, 1)

            def transposes2(n):
                pe.wait_ge(xn2_ready, n + 1)
                if has(n + 1):
                    pe.wait_ge(o_lo, 2 * n + 4)
                for k in range(KT):
                    for j in range(QT):
                        i = nc.tensor.transpose(BC0[:, k * S + j * P:k * S + j * P + P], xn2[:, j, k * P:(k + 1) * P],
                                                ident[:])
                i.then_inc(x2_done, 1)

            def logits(n):
                pe.wait_ge(x2_lo, n + 1)
                pe.wait_ge(gw_lo, 1)
                for j in range(QT):
                    i = product(BC0[:, j * E:(j + 1) * E], lambda a, k: x2T[:, a, k, j * P:(j + 1) * P],
                                lambda a, k: gw_s[:, a, k], range(KT))
                i.then_inc(l_done, 1)

            def rows_in(t, p):
                pe.wait_ge(x_loaded[p], (t // 2 + 1) * 16 if isinstance(t, int) else t * 8 + (16 - 8 * p))
                if isinstance(t, int) and t == 0:
                    pe.wait_ge(o_lo, 2 * B - 1)
                else:
                    pe.wait_ge(tx_lo, t)
                for k in range(KT):
                    for j in range(QT):
                        i = nc.tensor.transpose(TXB[:, k * R + j * P:k * R + j * P + P], xin[:, p, j, k * P:(k + 1) * P],
                                                ident[:])
                i.then_inc(tx_done, 1)

            def gate_up(t, p, h, routed):
                pe.wait_ge(w_lo[h], cuts(t, routed))
                pe.wait_ge(tx_lo, t + 1)
                if not isinstance(t, int) or t >= 1:
                    pe.wait_ge(h_ready, t * 2 + h - 1)
                for c, bank in ((0, GATE[h]), (1, UP[h])):
                    for m in range(KD // 2):
                        i = product(bank[:, m * R:(m + 1) * R],
                                    lambda a, k: wgu[h][:, a, c * KT + k, m * P:(m + 1) * P],
                                    lambda a, k: tx[p][:, a, k], range(KT))
                i.then_inc(gu_done, 1)

            def step(b):
                if has(b - 1):
                    turn(b - 1)
                if has(b):
                    scores(b)
                if has(b + 1):
                    transposes(b + 1)
                if has(b - 1):
                    attend(b - 1)
                if is_last(b):
                    rows_in(0, 0)
                if has(b) and has(b - 1):
                    values(b)
                if has(b + 1):
                    context_transposes(b + 1)
                    projections(b + 1)
                if has(b - 2):
                    transposes2(b - 2)
                if has(b + 1):
                    projected_keys(b + 1)
                if has(b - 1):
                    project_out(b - 1)
                if is_last(b):
                    gate_up(0, 0, 0, False)
                if has(b - 2):
                    logits(b - 2)

            transposes(0)
            context_transposes(0)
            projections(0)
            projected_keys(0)
            values(0)
            over_batches(pe, step)
            gate_up(0, 0, 1, False)
            transposes2(B - 1)
            logits(B - 1)

            def count_prefixes():
                pe.wait_ge(mask_ready, 1)
                m = mask[:].rearrange("p t e -> p (t e)")
                nc.tensor.matmul(BE[:, 0:T * E], before[:], m, start=True, stop=True)
                nc.tensor.matmul(BE[:, T * E:2 * T * E], ones[:], m, start=True, stop=True).then_inc(prefix_done, 1)

            def down(t, h, routed):
                pe.wait_ge(w_lo[2 + h], cuts(t, routed))
                pe.wait_ge(h_lo, t * 2 + h + 1)
                if isinstance(t, int) and t == 0 and h == 0:
                    pe.wait_ge(l_ready, B)
                elif h == 0:
                    pe.wait_ge(y_ready, t)
                for j in range(QT):
                    for m in range(KD // 2):
                        for u, (a, c) in enumerate(PASSES):
                            i = nc.tensor.matmul(YB[j], hs[h][:, a, m, j * P:(j + 1) * P], wdn[h][:, c, m],
                                                 start=(h == 0 and m == 0 and u == 0),
                                                 stop=(h == 1 and m == KD // 2 - 1 and u == 2))
                i.then_inc(d_done, 1)

            def tile(t, p, routed):
                late = isinstance(t, int) and t == SHARED - 1
                if exists(t + 1) and not late:
                    rows_in(t + 1, 1 - p)
                if not isinstance(t, int) or t > 0:
                    gate_up(t, p, 1, routed(0))
                down(t, 0, routed(0))
                if isinstance(t, int) and t == 1:
                    count_prefixes()
                if late:
                    rows_in(t + 1, 1 - p)
                if exists(t + 1):
                    gate_up(t + 1, 1 - p, 0, routed(1))
                down(t, 1, routed(0))

            over_tiles(pe, tile)


_INS = ['x', 'ctx_768', 'g_xattn', 'g_ffn', 'L0_xattn_Wq', 'L0_xattn_Wk', 'L0_xattn_Wv', 'L0_xattn_Wout',
        'L0_xattn_bout', 'L0_ffn_gate_w', 'L0_ffn_w_gate', 'L0_ffn_w_up', 'L0_ffn_w_down', 'L0_ffn_ws_gate',
        'L0_ffn_ws_up', 'L0_ffn_ws_down']
_OUT = (8, 256, 256)
_SPARE = 256


def kernel(**inputs):
    import numpy as _np
    import concourse.bacc as _bacc
    from concourse import mybir as _mybir
    from concourse.bass_utils import run_bass_kernel_spmd as _run

    nc = _bacc.Bacc("TRN2", target_bir_lowering=False, num_devices=1)
    arrays, args = {}, []
    for name in _INS:
        a = _np.ascontiguousarray(inputs[name])
        arrays[f"in_{name}_dram"] = a
        args.append(nc.dram_tensor(f"in_{name}_dram", a.shape, _mybir.dt.from_np(a.dtype), kind="ExternalInput").ap())
    out = nc.dram_tensor("out_dram", (_OUT[0] * _OUT[1] + _SPARE, _OUT[2]), _mybir.dt.float32, kind="ExternalOutput").ap()
    build(nc, *args, out)
    r = _run(nc, [arrays], core_ids=[0])
    return r.results[0]["out_dram"][:_OUT[0] * _OUT[1]].reshape(_OUT)
```

```python
from contextlib import ExitStack

import concourse.bass as bass
from concourse import mybir

F32 = mybir.dt.float32
F32R = mybir.dt.float32r
U32 = mybir.dt.uint32
I32 = mybir.dt.int32
ALU = mybir.AluOpType
ACT = mybir.ActivationFunctionType
AX = mybir.AxisListType

P = 128
HEADS = 8
DH = 64
PAIRS = HEADS // 2
EPS = 1e-5

HI, LO = 0, 1
PASSES = ((HI, HI), (HI, LO), (LO, HI))


def build(nc, x, ctx_in, g_xattn, g_ffn, wq, wk, wv, wo, bout, gate_w, w_gate, w_up, w_down,
          ws_gate, ws_up, ws_down, out):
    B, S, H = x.shape
    _, M, C = ctx_in.shape
    INNER = HEADS * DH
    KT = H // P
    CT = 2
    CP = C // CT
    QT = S // P
    MT = INNER // P
    T = B * QT
    SCALE = DH ** -0.5

    N = B * S
    E, _, D = w_gate.shape
    KD = D // P
    TOP = 2
    R = QT * P
    SHARED = N // R
    ROUTED = N * TOP // R + E - 1
    TILES = SHARED + ROUTED
    SLOT_STEPS = 2 + 2 * 4
    LAST_PAIR = TILES // 2 * 2 - 2
    CUTS = SHARED - 2
    RW = H + 2
    IDC, WC = H, H + 1
    GW = 2 * KT * D
    RAW = GW + KD * H
    EARLY = 6

    xg = nc.dram_tensor("xg", (ROUTED * R, RW), F32, kind="Internal").ap()

    es = ExitStack()
    early = ExitStack()
    with es:
        def sb(name, shape, dt=F32):
            return es.enter_context(nc.sbuf_tensor(name, shape, dt))

        def sb_attn(name, shape, dt=F32):
            return early.enter_context(nc.sbuf_tensor(name, shape, dt))

        def sem(name):
            return es.enter_context(nc.semaphore(name))

        psum = es.enter_context(nc.psum_tensor("psum", [P, 8, 512], F32))
        SCORES = [psum[:, 0:2], psum[:, 2:4]]
        TURNED = [psum[:, 6:8], psum[:, 4:6]]
        BA0, BA1, BB0, BB1, BC0, BC1, BD, BE = (psum[:, n] for n in range(8))

        GATE, UP = [psum[:, 0], psum[:, 2]], [psum[:, 1], psum[:, 3]]
        YB, TXB = [psum[:, 4, 0:H], psum[:, 5, 0:H]], psum[:, 6]

        ident = sb("ident", [P, P])
        half = sb("half", [P, QT])
        gx = sb("gx", [P, 2])
        tg = sb("tg", [P, 2])
        xr = [sb(f"xr{k}", [P, T, RW]) for k in range(TOP)]
        xn2 = sb("xn2", [P, QT, H])
        x2T = sb("x2T", [P, 2, KT, S], F32R)
        gw_raw = sb("gw_raw", [P, KT, E])
        gw_s = sb("gw_s", [P, 2, KT, E], F32R)
        stats2 = sb("stats2", [P, QT, 6])
        mv2 = sb("mv2", [P, QT, 2])
        vare2 = sb("vare2", [P, QT])
        rstd2 = sb("rstd2", [P, QT])
        logit = sb("logit", [P, T, E])
        ones = sb("ones", [P, P])
        before = sb("before", [P, P])
        first = sb("first", [P, E])
        more = sb("more", [P, E, E])
        count_i = sb("count_i", [P, ROUTED], I32)
        count = sb("count", [P, ROUTED])
        count_r = sb("count_r", [P, E])
        etab = sb("etab", [1, ROUTED + 2], I32)
        pos = sb("pos", [P, TOP, T], U32)
        pad = sb("pad", [P, QT, RW])

        crow = sb_attn("crow", [M, 2, C])
        wv_s = sb_attn("wv_s", [CP, 2, CT, INNER], F32R)
        wq_s = sb_attn("wq_s", [P, 2, KT, INNER], F32R)
        wk_s = sb_attn("wk_s", [CP, 2, CT, INNER], F32R)

        stats = sb_attn("stats", [P, QT, 6])
        mv = sb_attn("mv", [P, QT, 2])
        vare = sb_attn("vare", [P, QT])
        rstd = sb_attn("rstd", [P, QT])
        xn = sb_attn("xn", [P, QT, H])
        xT = sb_attn("xT", [P, 2, KT, S], F32R)
        cT = sb_attn("cT", [CP, 2, CT, 2 * M], F32R)
        bias = sb_attn("bias", [P, H])
        qT = sb_attn("qT", [P, 2, MT, S], F32R)
        kz = sb_attn("kz", [P, 2, PAIRS, 2, 2, M], F32R)
        vz = sb_attn("vz", [M, 2, HEADS, P], F32R)
        prob = sb_attn("prob", [P, QT, HEADS, M])
        mx = sb_attn("mx", [P, QT, HEADS])
        den = sb_attn("den", [P, QT, HEADS])
        rden = sb_attn("rden", [P, QT, HEADS])
        pT = sb_attn("pT", [M, 2, HEADS, S], F32R)
        oT = sb_attn("oT", [P, 2, PAIRS, S], F32R)
        wo_s = sb_attn("wo_s", [P, 2, MT, H], F32R)
        rows = sb_attn("rows", [P, T, H])
        wstage = xr[0][:].rearrange("p t c -> p (t c)")[:, 0:4 * 1024].rearrange("p (n c) -> p n c", n=4)
        early.close()

        wgu = [sb(f"wgu{h}", [P, 2, 2 * KT, D // 2], F32R) for h in range(2)]
        wdn = [sb(f"wdn{h}", [P, 2, KD // 2, H], F32R) for h in range(2)]
        xin = sb("xin", [P, 2, QT, RW])
        tx = [sb(f"tx{n}", [P, 2, KT, R], F32R) for n in range(2)]
        meta = sb("meta", [P, 2, QT, 2])
        hid = sb("hid", [P, 2, 2 * R])
        hs = [sb(f"hs{h}", [P, 2, KD // 2, R], F32R) for h in range(2)]
        ys = sb("ys", [P, 2, QT, H])

        small = [sb_attn(f"small{n}", [P, T]) for n in range(7)]
        slot_f = [sb_attn(f"slot_f{k}", [P, T]) for k in range(TOP)]
        score = sb_attn("score", [P, T, E])
        shift = sb_attn("shift", [P, T, E])
        sel = [sb_attn(f"sel{k}", [P, T, E]) for k in range(TOP)]
        mask = sb_attn("mask", [P, T, E])
        inside = sb_attn("inside", [P, T, E])
        total = sb_attn("total", [P, T, E])
        cum = [sb_attn(f"cum{n}", [P, T, E]) for n in range(2)]
        slot = sb_attn("slot", [P, T, E])
        picked = [sb_attn(f"picked{k}", [P, T, E]) for k in range(TOP)]
        tokens_e = sb_attn("tokens_e", [P, E])
        square = sb_attn("square", [P, E, E])
        square2 = sb_attn("square2", [P, E, E])
        tiles_e = sb_attn("tiles_e", [P, E])
        base_e = sb_attn("base_e", [P, E])
        owner = sb_attn("owner", [1, ROUTED, E])
        owner_f = sb_attn("owner_f", [1, ROUTED])
        equal = sb_attn("equal", [P, T, E])
        rest = sb_attn("rest", [P, T, E])
        early.close()
        raw = sb("raw", [P, E + 1, RAW])

        s_x = sem("s_x")
        s_c = sem("s_c")
        s_g = sem("s_g")
        s_b = sem("s_b")
        s_w = [sem(f"s_w{n}") for n in range(4)]
        ident_ready = sem("ident_ready")
        const_ready = sem("const_ready")
        zero_ready = sem("zero_ready")
        tanh_ready = sem("tanh_ready")
        bias_ready = sem("bias_ready")
        whi_ready = sem("whi_ready")
        wlo_ready = sem("wlo_ready")
        stat_step = sem("stat_step")
        stat_ready = sem("stat_ready")
        stat_passed = sem("stat_passed")
        var_passed = sem("var_passed")
        rstd_step = sem("rstd_step")
        rstd_ready = sem("rstd_ready")
        xn_ready = sem("xn_ready")
        biased = sem("biased")
        xT_done, xT_hi, xT_lo = sem("xT_done"), sem("xT_hi"), sem("xT_lo")
        cT_done, cT_hi, cT_lo = sem("cT_done"), sem("cT_hi"), sem("cT_lo")
        q_done, q_hi, q_lo = sem("q_done"), sem("q_hi"), sem("q_lo")
        k_done, k_hi, k_lo = sem("k_done"), sem("k_hi"), sem("k_lo")
        v_done, v_hi, v_lo = sem("v_done"), sem("v_hi"), sem("v_lo")
        s_done = sem("s_done")
        max_ready, exp_ready = sem("max_ready"), sem("exp_ready")
        rden_ready, norm_ready = sem("rden_ready"), sem("norm_ready")
        p_done, p_hi, p_lo = sem("p_done"), sem("p_hi"), sem("p_lo")
        o_done, o_hi, o_lo = sem("o_done"), sem("o_hi"), sem("o_lo")
        y_done, y_added = sem("y_done"), sem("y_added")
        s_rows = sem("s_rows")
        s_x0 = sem("s_x0")
        sp_passed = sem("sp_passed")
        s_res = [sem(f"s_res{n}") for n in range(2)]
        s_stored = [sem(f"s_stored{n}") for n in range(2)]
        s_pad = sem("s_pad")
        s_zero = sem("s_zero")
        s_raw = [sem(f"s_raw{e}") for e in range(E + 1)]
        s_slots = sem("s_slots")
        x_loaded = [sem(f"x_loaded{n}") for n in range(2)]
        s_added = sem("s_added")
        pad_ready, id_ready = sem("pad_ready"), sem("id_ready")
        s_gw, gw_hi, gw_lo = sem("s_gw"), sem("gw_hi"), sem("gw_lo")
        stat2_step, stat2_ready, stat2_passed = sem("stat2_step"), sem("stat2_ready"), sem("stat2_passed")
        rstd2_step, rstd2_ready = sem("rstd2_step"), sem("rstd2_ready")
        xn2_ready, row0_ready, row1_ready = sem("xn2_ready"), sem("row0_ready"), sem("row1_ready")
        x2_done, x2_hi, x2_lo = sem("x2_done"), sem("x2_hi"), sem("x2_lo")
        l_done, l_ready = sem("l_done"), sem("l_ready")
        route_step = sem("route_step")
        shifted, expd = sem("shifted"), sem("expd")
        mask_ready, prefix_done = sem("mask_ready"), sem("prefix_done")
        counts_ready, slot_step = sem("counts_ready"), sem("slot_step")
        sum_ready, weight_ready = sem("sum_ready"), sem("weight_ready")
        pos_ready, etab_ready = sem("pos_ready"), sem("etab_ready")
        tx_done, tx_hi, tx_lo = sem("tx_done"), sem("tx_hi"), sem("tx_lo")
        gu_done, silu_ready, h_ready = sem("gu_done"), sem("silu_ready"), sem("h_ready")
        h_hi, h_lo = sem("h_hi"), sem("h_lo")
        d_done, y_ready = sem("d_done"), sem("y_ready")
        w_hi = [sem(f"w_hi{g}") for g in range(4)]
        w_lo = [sem(f"w_lo{g}") for g in range(4)]
        meta_ready, pool_passed = sem("meta_ready"), sem("pool_passed")

        def f32(ap):
            return ap.bitcast(F32)

        def flat(ap):
            return ap.rearrange("p a b -> p (a b)")

        def key_sums(r):
            return psum[r, 2:4, 0:4 * M].rearrange("p c (n k) -> p c n k", k=M)

        def keys(r, part, a):
            return kz[r, part, :, :, a].rearrange("p (c m) n k -> p c (m n) k", c=2)

        def group_raw(e, g):
            w = raw[:, bass.ds(e, 1)].squeeze(1)
            if g < 2:
                return w[:, 0:GW].rearrange("p (a n) -> p a n", n=D)[:, :, g * (D // 2):(g + 1) * (D // 2)]
            n = KD // 2 * H
            return w[:, GW + (g - 2) * n:GW + (g - 1) * n].rearrange("p (a n) -> p a n", n=H)

        def group_split(g, part):
            return (wgu[g] if g < 2 else wdn[g - 2])[:, part]

        def expert(eng, t):
            return eng.value_load(etab[0:1, bass.ds(t - SHARED, 1)], min_val=0, max_val=E - 1)

        def over_tiles(eng, step, routed_from_here=None):
            def peeled(t):
                step(t, t % 2, lambda d: t + d >= SHARED)

            peeled(0)
            peeled(1)
            with eng.Fori(1, SHARED // 2 - 1) as u:
                for p in range(2):
                    step(u * 2 + p, p, lambda d: False)
            if routed_from_here:
                routed_from_here()
            peeled(SHARED - 2)
            peeled(SHARED - 1)
            over_routed(eng, step)

        def over_routed(eng, step):
            with eng.Fori(SHARED // 2, LAST_PAIR // 2) as u:
                for p in range(2):
                    step(u * 2 + p, p, lambda d: True)
            for t in range(LAST_PAIR, TILES):
                step(t, t % 2, lambda d: True)

        def cuts(t, routed):
            return t - CUTS if routed else 1

        def has(n):
            return not isinstance(n, int) or 0 <= n < B

        def is_last(b):
            return isinstance(b, int) and b == B

        def more_context(g):
            return not isinstance(g, int) or g + 1 < B // 2

        def with_first_rows(b):
            return isinstance(b, int) and b == B - 1

        def rows_bank(t):
            return BC1 if isinstance(t, int) and t == 0 else TXB

        def over_batches(eng, step, before_last=None):
            def peeled(b):
                step(b, b % 2, b // 2)

            peeled(0)
            peeled(1)
            with eng.Fori(1, B // 2 - 1) as g:
                for n in range(2):
                    step(g * 2 + n, n, g)
            for b in range(B - 2, B + 1):
                if b == B and before_last:
                    before_last()
                peeled(b)

        def exists(t):
            return not isinstance(t, int) or t < TILES

        block = es.enter_context(nc.Block())

        @block.sync
        def _(sp):
            def load_expert(sp, e):
                gate, up, down = (w_gate[e], w_up[e], w_down[e]) if e < E else (ws_gate, ws_up, ws_down)
                for n, w in enumerate((gate, up)):
                    sp.dma_start(raw[:, e, n * KT * D:(n + 1) * KT * D].rearrange("p (k d) -> p k d", d=D),
                                 w.rearrange("(k p) d -> p k d", p=P)).then_inc(s_raw[e], 16)
                sp.dma_start(raw[:, e, GW:RAW].rearrange("p (m h) -> p m h", h=H),
                             down.rearrange("(m p) h -> p m h", p=P)).then_inc(s_raw[e], 16)

            x_rows = x.rearrange("b (j p) h -> p (b j) h", p=P)
            sp.dma_start(rows[:, 0:QT], x_rows[:, 0:QT]).then_inc(s_x0, 16)

            def load_matrix(n, w, k):
                part = w.shape[0] // k
                sp.dma_start(wstage[0:part, n].rearrange("p (k n) -> p k n", k=k),
                             w.rearrange("(k p) n -> p k n", k=k)).then_inc(s_w[n], 16)

            def load_context(g):
                if g:
                    sp.wait_ge(cT_done, g)
                sp.dma_start(crow[:], ctx_in[2 * g:2 * g + 2].rearrange("b m c -> m b c")).then_inc(s_c, 16)

            load_matrix(0, wq, KT)
            load_context(0)
            load_matrix(1, wk, CT)
            sp.dma_start(rows[:, QT:T], x_rows[:, QT:T]).then_inc(s_x, 16)
            load_matrix(2, wv, CT)
            load_matrix(3, wo, MT)
            sp.dma_start(gw_raw[:], gate_w.rearrange("(k p) e -> p k e", p=P)).then_inc(s_gw, 16)
            load_context(1)
            for e in range(E, EARLY - 1, -1):
                load_expert(sp, e)
            sp.wait_ge(pad_ready, 2)
            with sp.Fori(0, ROUTED) as t:
                sp.dma_start(xg[bass.ds(t * R, R)].rearrange("(j p) c -> p j c", p=P), pad[:]).then_inc(s_pad, 16)
            sp.dma_start(out[N:N + R].rearrange("(j p) h -> p j h", p=P), pad[:, :, 0:H]).then_inc(s_zero, 16)

            def store_rows(b):
                sp.wait_ge(y_added, b + 1)
                sp.dma_start(out[bass.ds(b * S, S)].rearrange("(j p) h -> p j h", p=P),
                             rows[:, bass.ds(b * QT, QT)]).then_inc(s_rows, 16)

            def shared_rows(t):
                sp.dma_start(xin[:, t % 2, :, 0:H], xr[0][:, t * QT:(t + 1) * QT, 0:H]).then_inc(x_loaded[t % 2], 16)

            def residual(t):
                sp.dma_start(ys[:, t % 2], out[t * R:(t + 1) * R].rearrange("(j q) h -> q j h", q=P)) \
                    .then_inc(s_res[t % 2], 16)

            def slot_rows(start, p):
                sp.dma_start(xin[:, p], xg[bass.ds(start, R)].rearrange("(j q) c -> q j c", q=P)) \
                    .then_inc(x_loaded[p], 16)

            for b in range(B - 2):
                store_rows(b)
                if b % 2 == 0 and b // 2 + 2 < B // 2:
                    load_context(b // 2 + 2)
            sp.wait_ge(q_done, 2 * B)
            sp.wait_ge(k_done, B // 2)
            sp.wait_ge(xT_done, B)
            for t in range(2):
                sp.wait_ge(row0_ready, t + 1)
                shared_rows(t)
            store_rows(B - 2)
            store_rows(B - 1)
            sp.wait_ge(s_rows, 16 * B)
            residual(0)
            sp.wait_ge(row0_ready, B)
            later = {0: (5, 4), 1: (3,), 2: (2,), 3: (1,), 4: (0,)}
            for t in range(SHARED):
                sp.wait_ge(tx_done, t + 1)
                if t + 2 < SHARED:
                    shared_rows(t + 2)
                if t + 1 < SHARED:
                    if t >= 1:
                        sp.wait_ge(s_stored[(t + 1) % 2], 16 * ((t + 1) // 2))
                    residual(t + 1)
                for e in later.get(t, ()):
                    if e == 1:
                        sp.wait_ge(etab_ready, 1)
                        sp.wait_ge(weight_ready, 3)
                    load_expert(sp, e)
                if t == SHARED - 2:
                    sp.wait_ge(s_slots, 16 * TOP * T)
                    slot_rows(0, 0)
                    sp.wait_ge(tx_done, SHARED)
                    slot_rows(R, 1)
                sp.wait_ge(y_ready, t + 1)
                sp.dma_start(out[t * R:(t + 1) * R].rearrange("(j q) h -> q j h", q=P), ys[:, t % 2]) \
                    .then_inc(s_stored[t % 2], 16)

            def refill(t, p, routed):
                if exists(t + 2):
                    start = t * R + (2 * R - N)
                    if not isinstance(t, int):
                        start = sp.snap(start)
                    sp.wait_ge(tx_done, t + 1)
                    sp.sem_inc(sp_passed, 1)
                    sp.wait_ge(meta_ready, t - (SHARED - 1))
                    slot_rows(start, p)

            over_routed(sp, refill)
            sp.wait_ge(s_added, 16 * QT * ROUTED)

        @block.gpsimd
        def _(pool):
            nc.gpsimd.memset(ident[:], 0.0).then_inc(const_ready, 1)
            nc.gpsimd.memset(half[:], -0.5).then_inc(const_ready, 1)
            pool.wait_ge(const_ready, 2)
            nc.gpsimd.affine_select(out=ident[:], in_=ident[:], compare_op=ALU.not_equal, fill=1.0,
                                    base=0, pattern=[[-1, P]], channel_multiplier=1).then_inc(ident_ready, 1)
            pool.dma_start(gx[:, 0:1], g_xattn.partition_broadcast(P)).then_inc(s_g, 16)
            pool.dma_start(gx[:, 1:2], g_ffn.partition_broadcast(P)).then_inc(s_g, 16)
            pool.dma_start(bias[:], bout.partition_broadcast(P)).then_inc(s_b, 16)

            def prepare(n):
                pool.wait_ge(stat_ready, n + 1)
                pool.sem_inc(var_passed, 1)
                nc.gpsimd.tensor_scalar(vare[:], mv[:, :, 1], EPS, None, ALU.add).then_inc(rstd_step, 1)
                pool.wait_ge(rstd_step, n + 1)
                nc.gpsimd.tensor_tensor(rstd[:], vare[:], half[:], ALU.pow).then_inc(rstd_ready, 1)

            def prepare2(n):
                pool.wait_ge(stat2_ready, n + 1)
                pool.sem_inc(pool_passed, 1)
                nc.gpsimd.tensor_scalar(vare2[:], mv2[:, :, 1], EPS, None, ALU.add).then_inc(rstd2_step, 1)
                pool.wait_ge(rstd2_step, n + 1)
                nc.gpsimd.tensor_tensor(rstd2[:], vare2[:], half[:], ALU.pow).then_inc(rstd2_ready, 1)

            def keep_rows(n):
                pool.wait_ge(xn2_ready, n + 1)
                nc.gpsimd.tensor_copy(xr[1][:, bass.ds(n * QT, QT), 0:H], xn2[:]).then_inc(row1_ready, 1)

            def normalise(b, j):
                pool.wait_ge(rden_ready, QT * b + j + 1)
                nc.gpsimd.tensor_tensor(prob[:, j], prob[:, j], rden[:, j].unsqueeze(2).to_broadcast([P, HEADS, M]),
                                        ALU.mult).then_inc(norm_ready, 1)

            def add_bias(b):
                pool.wait_ge(xn_ready, b + 1)
                r = rows[:, bass.ds(b * QT, QT)]
                nc.gpsimd.tensor_tensor(r, r, bias[:].unsqueeze(1).to_broadcast([P, QT, H]),
                                        ALU.add).then_inc(biased, 1)

            def step(b, odd, g):
                if has(b - 2):
                    prepare2(b - 2)
                if has(b):
                    normalise(b, 0)
                if has(b - 2):
                    keep_rows(b - 2)
                if has(b + 2):
                    prepare(b + 2)
                if has(b):
                    normalise(b, 1)
                    add_bias(b)

            prepare(0)
            nc.gpsimd.memset(f32(kz[:]), 0.0).then_inc(zero_ready, 1)
            nc.gpsimd.memset(f32(vz[:]), 0.0).then_inc(zero_ready, 1)
            nc.gpsimd.memset(pad[:], 0.0).then_inc(pad_ready, 1)
            pool.wait_ge(pad_ready, 1)
            nc.gpsimd.iota(pad[:, :, IDC].bitcast(I32), pattern=[[P, QT]], base=N, channel_multiplier=1) \
                .then_inc(pad_ready, 1)

            nc.gpsimd.memset(ones[:], 1.0).then_inc(const_ready, 1)
            for t in (more, before):
                nc.gpsimd.memset(t[:], 1.0).then_inc(const_ready, 1)
            nc.gpsimd.iota(count_i[:], pattern=[[1, ROUTED]], base=0, channel_multiplier=0).then_inc(const_ready, 1)
            pool.wait_ge(const_ready, 6)
            nc.gpsimd.affine_select(out=more[:], in_=more[:], compare_op=ALU.is_gt, fill=0.0, base=0,
                                    pattern=[[-1, E], [1, E]], channel_multiplier=0).then_inc(const_ready, 1)
            nc.gpsimd.affine_select(out=before[:], in_=before[:], compare_op=ALU.is_gt, fill=0.0, base=0,
                                    pattern=[[1, P]], channel_multiplier=-1).then_inc(const_ready, 1)

            prepare(1)
            pool.wait_ge(s_b, 16)
            pool.wait_ge(tanh_ready, 1)
            nc.gpsimd.tensor_scalar(bias[:], bias[:], tg[:, 0:1], None, ALU.mult).then_inc(bias_ready, 1)
            pool.wait_ge(bias_ready, 1)
            over_batches(pool, step)

            for g in (1, 2):
                pool.wait_ge(w_hi[g], 1)
                nc.gpsimd.tensor_tensor(group_split(g, LO), group_raw(E, g), f32(group_split(g, HI)),
                                        ALU.subtract).then_inc(w_lo[g], 1)

            pool.wait_ge(wlo_ready, 4)
            for k in range(TOP):
                nc.gpsimd.iota(xr[k][:, :, IDC].bitcast(I32), pattern=[[P, T]], base=0, channel_multiplier=1) \
                    .then_inc(id_ready, 1)
            prepare2(B - 1)
            keep_rows(B - 1)

            slot_steps = 0
            src = total
            pool.wait_ge(counts_ready, 1)
            for n, d in enumerate((1, 2, 4, 8)):
                dst = cum[n % 2]
                nc.gpsimd.tensor_copy(dst[:, 0:d], src[:, 0:d]).then_inc(slot_step, 1)
                nc.gpsimd.tensor_tensor(dst[:, d:T], src[:, d:T], src[:, 0:T - d], ALU.add).then_inc(slot_step, 1)
                slot_steps += 2
                pool.wait_ge(slot_step, slot_steps)
                src = dst
            nc.gpsimd.tensor_tensor(slot[:], src[:], total[:], ALU.subtract).then_inc(slot_step, 1)
            pool.wait_ge(slot_step, slot_steps + 1)
            nc.gpsimd.tensor_tensor(slot[:], slot[:], inside[:], ALU.add).then_inc(slot_step, 1)

            top1, top2, part, scale = (small[n][:] for n in (0, 1, 4, 6))
            pool.wait_ge(sum_ready, 1)
            nc.gpsimd.tensor_scalar(scale, part, tg[:, 1:2], None, ALU.mult).then_inc(weight_ready, 1)
            pool.wait_ge(weight_ready, 1)
            nc.gpsimd.tensor_tensor(xr[0][:, :, WC], top1, scale, ALU.mult).then_inc(weight_ready, 1)
            nc.gpsimd.tensor_tensor(xr[1][:, :, WC], top2, scale, ALU.mult).then_inc(weight_ready, 1)

            pool.wait_ge(weight_ready, 3)
            pool.wait_ge(id_ready, TOP)
            pool.wait_ge(row0_ready, B)
            pool.wait_ge(row1_ready, B)
            pool.wait_ge(pos_ready, 1)
            pool.wait_ge(s_pad, 16 * ROUTED)
            for j in range(T):
                for k in range(TOP):
                    pool.indirect_dma_start(out=xg, out_offset=bass.IndirectOffsetOnAxis(ap=pos[:, k, j:j + 1], axis=0),
                                            in_=xr[k][:, j, :], in_offset=None).then_inc(s_slots, 16)

            def split_low(number, g, e):
                pool.wait_ge(w_hi[g], number)
                nc.gpsimd.tensor_tensor(group_split(g, LO), group_raw(e, g), f32(group_split(g, HI)),
                                        ALU.subtract).then_inc(w_lo[g], 1)

            def copy_meta(t, p):
                pool.wait_ge(x_loaded[p], (t // 2 + 1) * 16 if isinstance(t, int) else t * 8 + (16 - 8 * p))
                pool.sem_inc(pool_passed, 1)
                nc.gpsimd.tensor_copy(meta[:, p], xin[:, p, :, IDC:RW]).then_inc(meta_ready, 1)

            def tile(t, p, routed):
                if exists(t + 1):
                    e1 = expert(pool, t + 1)
                    split_low(cuts(t + 1, True), 1, e1)
                    split_low(cuts(t + 1, True), 2, e1)
                if not isinstance(t, int) or t > SHARED:
                    pool.wait_ge(s_added, t * (16 * QT) - 16 * QT * SHARED)
                    pool.sem_inc(pool_passed, 1)
                if exists(t + 1):
                    copy_meta(t + 1, 1 - p)
                pool.wait_ge(y_ready, t + 1)
                pool.sem_inc(pool_passed, 1)
                for j in range(QT):
                    pool.indirect_dma_start(
                        out=out, out_offset=bass.IndirectOffsetOnAxis(ap=meta[:, p, j, 0:1].bitcast(U32), axis=0),
                        in_=ys[:, p, j], in_offset=None, compute_op=ALU.add).then_inc(s_added, 16)

            pool.wait_ge(etab_ready, 1)
            for e in range(E):
                pool.wait_ge(s_raw[e], 48)
            e0 = expert(pool, SHARED)
            copy_meta(SHARED, 0)
            split_low(2, 1, e0)
            split_low(2, 2, e0)
            pool.wait_ge(s_zero, 16)
            for n in range(2):
                pool.wait_ge(s_stored[n], 16 * (SHARED // 2))
            tile(SHARED, 0, lambda d: d >= 0)
            tile(SHARED + 1, 1, lambda d: True)
            with pool.Fori(SHARED // 2 + 1, LAST_PAIR // 2) as u:
                for p in range(2):
                    tile(u * 2 + p, p, lambda d: True)
            for t in range(LAST_PAIR, TILES):
                tile(t, t % 2, lambda d: True)

        @block.scalar
        def _(act):
            def matrix_high(n):
                w, part = ((wq_s, P), (wk_s, CP), (wv_s, CP), (wo_s, P))[n]
                act.wait_ge(s_w[n], 16)
                nc.scalar.copy(w[:, HI].rearrange("p k n -> p (k n)"), wstage[0:part, n]).then_inc(whi_ready, 1)

            def transposed(n):
                act.wait_ge(xT_done, n + 1)
                nc.scalar.copy(xT[:, HI].rearrange("p k s -> p (k s)"), BC1).then_inc(xT_hi, 1)

            def transposed_context(n):
                act.wait_ge(cT_done, n + 1)
                nc.scalar.copy(cT[:, HI].rearrange("p k s -> p (k s)"), BC1[0:CP, 0:CT * 2 * M]).then_inc(cT_hi, 1)

            def projected(n, i):
                act.wait_ge(q_done, 2 * n + i + 1)
                nc.scalar.mul(qT[:, HI, 2 * i:2 * i + 2].rearrange("p k s -> p (k s)"), (BA0, BA1)[i], SCALE) \
                    .then_inc(q_hi, 1)

            def projected_keys(n):
                act.wait_ge(k_done, n + 1)
                act.wait_ge(zero_ready, 1)
                for a in range(2):
                    r = slice(a * DH, (a + 1) * DH)
                    nc.scalar.copy(keys(r, HI, a), key_sums(r)).then_inc(k_hi, 1)

            def exp(b, j):
                act.wait_ge(max_ready, QT * b + j + 1)
                sc = SCORES[j][:, :, 0:4 * M].rearrange("p c (h k) -> p c h k", k=M)
                for h in range(HEADS):
                    i = nc.scalar.activation(prob[:, j, h], sc[:, h // 4, h % 4], ACT.Exp, bias=mx[:, j, h:h + 1],
                                             accum_out=den[:, j, h:h + 1])
                i.then_inc(exp_ready, 1)

            def values(b):
                act.wait_ge(v_done, b + 1)
                act.wait_ge(zero_ready, 2)
                v = vz[:, HI].rearrange("p (g a) (c d) -> p g (a c) d", a=2, c=2)[:, :, 0:4:3]
                nc.scalar.copy(v, BE[0:M].rearrange("p (g a d) -> p g a d", g=PAIRS, a=2)).then_inc(v_hi, 1)

            def turned(b):
                for i in range(2):
                    act.wait_ge(p_done, 2 * b + i + 1)
                    nc.scalar.copy(pT[:, HI, 4 * i:4 * i + 4].rearrange("p (c h) s -> p c (h s)", c=2),
                                   TURNED[i][0:M]).then_inc(p_hi, 1)

            def attended(b, i):
                act.wait_ge(o_done, 2 * b + i + 1)
                nc.scalar.copy(oT[:, HI, 2 * i:2 * i + 2].rearrange("p k s -> p (k s)"), (BD, BC0)[i]).then_inc(o_hi, 1)

            def normed(n):
                act.wait_ge(x2_done, n + 1)
                nc.scalar.copy(flat(x2T[:, HI]), BC0).then_inc(x2_hi, 1)

            def keep_rows(n):
                act.wait_ge(xn2_ready, n + 1)
                nc.scalar.copy(xr[0][:, bass.ds(n * QT, QT), 0:H], xn2[:]).then_inc(row0_ready, 1)

            def split_high(g, e):
                nc.scalar.copy(group_split(g, HI), group_raw(e, g)).then_inc(w_hi[g], 1)

            def rows_high(t, p):
                act.wait_ge(tx_done, t + 1)
                nc.scalar.copy(flat(tx[p][:, HI]), rows_bank(t)).then_inc(tx_hi, 1)

            def silu(t, h):
                act.wait_ge(gu_done, t * 2 + h + 1)
                nc.scalar.activation(hid[:, h], GATE[h], ACT.Silu).then_inc(silu_ready, 1)

            def hidden_high(t, h):
                act.wait_ge(h_ready, t * 2 + h + 1)
                nc.scalar.copy(flat(hs[h][:, HI]), hid[:, h]).then_inc(h_hi, 1)

            def step(b, odd, g):
                if has(b - 1):
                    turned(b - 1)
                if has(b + 1):
                    transposed(b + 1)
                if has(b):
                    exp(b, 0)
                if has(b - 1):
                    attended(b - 1, 0)
                    attended(b - 1, 1)
                if with_first_rows(b):
                    rows_high(0, 0)
                if is_last(b):
                    act.wait_ge(biased, B)
                    silu(0, 0)
                if odd and more_context(g):
                    transposed_context(g + 1)
                if has(b):
                    exp(b, 1)
                    values(b)
                if has(b - 2):
                    keep_rows(b - 2)
                if has(b + 1):
                    projected(b + 1, 0)
                if has(b - 2):
                    normed(b - 2)
                if has(b + 1):
                    projected(b + 1, 1)
                if odd and more_context(g):
                    projected_keys(g + 1)

            def shared_high():
                act.wait_ge(s_raw[E], 48)
                for g in range(4):
                    split_high(g, E)

            matrix_high(0)
            transposed(0)
            matrix_high(1)
            transposed_context(0)
            act.wait_ge(s_g, 32)
            nc.scalar.activation(tg[:], gx[:], ACT.Tanh).then_inc(tanh_ready, 1)
            projected(0, 0)
            projected(0, 1)
            matrix_high(2)
            projected_keys(0)
            matrix_high(3)
            act.wait_ge(s_gw, 16)
            nc.scalar.copy(gw_s[:, HI], gw_raw[:]).then_inc(gw_hi, 1)
            over_batches(act, step, shared_high)
            hidden_high(0, 0)
            rows_high(1, 1)
            silu(0, 1)
            keep_rows(B - 1)
            normed(B - 1)
            hidden_high(0, 1)
            act.wait_ge(h_lo, 1)
            silu(1, 0)

            def tile(t, p, routed):
                e1 = expert(act, t + 1) if exists(t + 1) and routed(1) else None
                e2 = expert(act, t + 2) if exists(t + 2) and routed(2) else None
                late = isinstance(t, int) and t == SHARED - 1
                begun = isinstance(t, int) and t == 0
                if exists(t + 1) and not late and not begun:
                    rows_high(t + 1, 1 - p)
                if begun:
                    act.wait_ge(shifted, 1)
                    nc.scalar.activation(score[:], shift[:], ACT.Exp).then_inc(expd, 1)
                else:
                    silu(t, 1)
                if late:
                    rows_high(t + 1, 1 - p)
                if isinstance(t, int) and t == 1:
                    act.wait_ge(prefix_done, 1)
                    nc.scalar.copy(flat(inside[:]), BE[:, 0:T * E])
                    nc.scalar.copy(flat(total[:]), BE[:, T * E:2 * T * E]).then_inc(counts_ready, 1)
                if e1 is not None:
                    split_high(1, e1)
                if not begun:
                    hidden_high(t, 1)
                if e1 is not None:
                    act.wait_ge(d_done, t * 2 + 1)
                    split_high(2, e1)
                if exists(t + 1):
                    if begun:
                        act.wait_ge(d_done, 1)
                    else:
                        silu(t + 1, 0)
                    if e2 is not None:
                        split_high(0, e2)
                    hidden_high(t + 1, 0)
                if e1 is not None:
                    act.wait_ge(d_done, t * 2 + 2)
                    split_high(3, e1)

            def all_weights():
                act.wait_ge(etab_ready, 1)
                for e in range(E):
                    act.wait_ge(s_raw[e], 48)

            over_tiles(act, tile, all_weights)

        @block.vector
        def _(dve):
            def low(dst, src, hi, done):
                nc.vector.tensor_tensor(dst, src, hi, ALU.subtract).then_inc(done, 1)

            def matrix_low(n):
                w, part = ((wq_s, P), (wk_s, CP), (wv_s, CP), (wo_s, P))[n]
                dve.wait_ge(whi_ready, n + 1)
                low(flat(w[:, LO]), wstage[0:part, n], flat(f32(w[:, HI])), wlo_ready)

            def statistics(n):
                for j in range(QT):
                    nc.vector.bn_stats(stats[:, j], rows[:, bass.ds(n * QT + j, 1)].squeeze(1)).then_inc(stat_step, 1)
                dve.wait_ge(stat_step, QT * n + QT)
                dve.sem_inc(stat_passed, 1)
                for j in range(QT):
                    i = nc.vector.bn_aggr(mv[:, j], stats[:, j])
                i.then_inc(stat_ready, 1)

            def layer_norm(n):
                dve.wait_ge(stat_ready, n + 1)
                dve.wait_ge(rstd_ready, n + 1)
                if has(n - 1):
                    dve.wait_ge(xT_done, n)
                for j in range(QT):
                    i = nc.vector.tensor_scalar(xn[:, j], rows[:, bass.ds(n * QT + j, 1)].squeeze(1), mv[:, j, 0:1],
                                                rstd[:, j:j + 1], ALU.subtract, ALU.mult)
                i.then_inc(xn_ready, 1)

            def transposed(n):
                dve.wait_ge(xT_hi, n + 1)
                low(flat(xT[:, LO]), BC1, flat(f32(xT[:, HI])), xT_lo)

            def transposed_context(n):
                dve.wait_ge(cT_hi, n + 1)
                low(flat(cT[:, LO]), BC1[0:CP, 0:CT * 2 * M], flat(f32(cT[:, HI])), cT_lo)

            def projected(n, i):
                dve.wait_ge(q_hi, 2 * n + i + 1)
                part = slice(2 * i, 2 * i + 2)
                nc.vector.scalar_tensor_tensor(
                    out=flat(qT[:, LO, part]), in0=(BA0, BA1)[i], scalar=SCALE, in1=flat(f32(qT[:, HI, part])),
                    op0=ALU.mult, op1=ALU.subtract).then_inc(q_lo, 1)

            def projected_keys(g, a):
                dve.wait_ge(k_hi, 2 * g + a + 1)
                r = slice(a * DH, (a + 1) * DH)
                nc.vector.tensor_tensor(keys(r, LO, a), key_sums(r), f32(keys(r, HI, a)), ALU.subtract) \
                    .then_inc(k_lo, 1)

            def maximum(b, j):
                dve.wait_ge(s_done, QT * b + j + 1)
                sc = SCORES[j][:, :, 0:4 * M].rearrange("p c (h k) -> p c h k", k=M)
                nc.vector.tensor_reduce(mx[:, j].rearrange("p (c h) -> p c h", c=2), sc, AX.X, ALU.max,
                                        negate=True).then_inc(max_ready, 1)

            def denominator(b, j):
                dve.wait_ge(exp_ready, QT * b + j + 1)
                nc.vector.reciprocal(rden[:, j], den[:, j]).then_inc(rden_ready, 1)

            def values(b):
                dve.wait_ge(v_hi, b + 1)
                v = [vz[:, w].rearrange("p (g a) (c d) -> p g (a c) d", a=2, c=2)[:, :, 0:4:3] for w in (HI, LO)]
                low(v[LO], BE[0:M].rearrange("p (g a d) -> p g a d", g=PAIRS, a=2), f32(v[HI]), v_lo)

            def turned(b):
                for i in range(2):
                    dve.wait_ge(p_hi, 2 * b + i + 1)
                    q = [pT[:, w, 4 * i:4 * i + 4].rearrange("p (c h) s -> p c (h s)", c=2) for w in (HI, LO)]
                    low(q[LO], TURNED[i][0:M], f32(q[HI]), p_lo)

            def attended(b):
                for i, bank in enumerate((BD, BC0)):
                    dve.wait_ge(o_hi, 2 * b + i + 1)
                    part = slice(2 * i, 2 * i + 2)
                    low(flat(oT[:, LO, part]), bank, flat(f32(oT[:, HI, part])), o_lo)

            def add(b):
                dve.wait_ge(y_done, b + 1)
                dve.wait_ge(biased, b + 1)
                r = flat(rows[:, bass.ds(b * QT, QT)])
                nc.vector.scalar_tensor_tensor(out=r, in0=BC1, scalar=tg[:, 0:1], in1=r, op0=ALU.mult,
                                               op1=ALU.add).then_inc(y_added, 1)

            def statistics2(n):
                dve.wait_ge(y_added, n + 1)
                dve.sem_inc(stat2_passed, 1)
                for j in range(QT):
                    nc.vector.bn_stats(stats2[:, j], rows[:, bass.ds(n * QT + j, 1)].squeeze(1)).then_inc(stat2_step, 1)
                dve.wait_ge(stat2_step, QT * n + QT)
                dve.sem_inc(stat2_passed, 1)
                for j in range(QT):
                    i = nc.vector.bn_aggr(mv2[:, j], stats2[:, j])
                i.then_inc(stat2_ready, 1)

            def layer_norm2(n):
                dve.wait_ge(stat2_ready, n + 1)
                dve.wait_ge(rstd2_ready, n + 1)
                for j in range(QT):
                    i = nc.vector.tensor_scalar(xn2[:, j], rows[:, bass.ds(n * QT + j, 1)].squeeze(1), mv2[:, j, 0:1],
                                                rstd2[:, j:j + 1], ALU.subtract, ALU.mult)
                i.then_inc(xn2_ready, 1)

            def normed(n):
                dve.wait_ge(x2_hi, n + 1)
                low(flat(x2T[:, LO]), BC0, flat(f32(x2T[:, HI])), x2_lo)

            def logits(n):
                dve.wait_ge(l_done, n + 1)
                nc.vector.tensor_copy(logit[:, bass.ds(n * QT, QT)], BC0[:, 0:QT * E].rearrange("p (j e) -> p j e", e=E)) \
                    .then_inc(l_ready, 1)

            def rows_low(t, p):
                dve.wait_ge(tx_hi, t + 1)
                low(flat(tx[p][:, LO]), rows_bank(t), flat(f32(tx[p][:, HI])), tx_lo)

            def split_low(number, g, e):
                dve.wait_ge(w_hi[g], number)
                low(group_split(g, LO), group_raw(e, g), f32(group_split(g, HI)), w_lo[g])

            def hidden(t, h):
                dve.wait_ge(silu_ready, t * 2 + h + 1)
                nc.vector.tensor_tensor(hid[:, h], hid[:, h], UP[h], ALU.mult).then_inc(h_ready, 1)

            def hidden_low(t, h):
                dve.wait_ge(h_hi, t * 2 + h + 1)
                low(flat(hs[h][:, LO]), hid[:, h], flat(f32(hs[h][:, HI])), h_lo)

            def step(b, odd, g):
                if has(b - 1):
                    turned(b - 1)
                if has(b):
                    maximum(b, 0)
                    maximum(b, 1)
                if has(b + 1):
                    transposed(b + 1)
                if has(b - 2):
                    layer_norm2(b - 2)
                if has(b):
                    denominator(b, 0)
                if has(b - 1):
                    attended(b - 1)
                if with_first_rows(b):
                    rows_low(0, 0)
                if is_last(b):
                    hidden(0, 0)
                if odd and more_context(g):
                    transposed_context(g + 1)
                if has(b + 2):
                    statistics(b + 2)
                if has(b):
                    denominator(b, 1)
                    values(b)
                if has(b + 1):
                    projected(b + 1, 0)
                if has(b - 2):
                    normed(b - 2)
                if has(b + 1):
                    projected(b + 1, 1)
                if odd and more_context(g):
                    projected_keys(g + 1, 0)
                if has(b - 1):
                    add(b - 1)
                if odd and more_context(g):
                    projected_keys(g + 1, 1)
                if has(b - 2) and not is_last(b):
                    logits(b - 2)
                if has(b - 1):
                    statistics2(b - 1)
                if with_first_rows(b):
                    split_low(1, 0, E)
                if is_last(b):
                    hidden_low(0, 0)
                    rows_low(1, 1)
                    split_low(1, 3, E)
                if has(b + 2):
                    layer_norm(b + 2)

            dve.wait_ge(s_x0, 16)
            statistics(0)
            layer_norm(0)
            matrix_low(0)
            transposed(0)
            matrix_low(1)
            transposed_context(0)
            projected(0, 0)
            projected(0, 1)
            dve.wait_ge(s_x, 16)
            statistics(1)
            matrix_low(2)
            projected_keys(0, 0)
            projected_keys(0, 1)
            layer_norm(1)
            matrix_low(3)
            dve.wait_ge(gw_hi, 1)
            low(gw_s[:, LO], gw_raw[:], f32(gw_s[:, HI]), gw_lo)
            dve.wait_ge(tanh_ready, 1)
            dve.sem_inc(l_ready, 1)
            over_batches(dve, step)
            layer_norm2(B - 1)
            logits(B - 2)
            hidden(0, 1)
            normed(B - 1)
            hidden_low(0, 1)
            hidden(1, 0)
            logits(B - 1)

            steps = [0]

            def then(i):
                steps[0] += 1
                i.then_inc(route_step, 1)
                dve.wait_ge(route_step, steps[0])

            V = nc.vector
            s0, s1, s2, s3, s4, s5, _ = (t[:] for t in small)

            def over_e(ap):
                return ap.unsqueeze(2).to_broadcast([P, T, E])

            dve.wait_ge(l_ready, B + 1)
            then(V.tensor_reduce(s0, logit[:], AX.X, ALU.max))
            V.tensor_tensor(shift[:], logit[:], over_e(s0), ALU.subtract).then_inc(shifted, 1)

            def best(k, src, top):
                then(V.tensor_reduce(top, src[:], AX.X, ALU.max))
                then(V.tensor_tensor(equal[:], src[:], over_e(top), ALU.is_equal))
                then(V.tensor_tensor(equal[:], equal[:], first[:].unsqueeze(1).to_broadcast([P, T, E]), ALU.mult))
                then(V.tensor_reduce(s5, equal[:], AX.X, ALU.max))
                then(V.tensor_tensor(sel[k][:], equal[:], over_e(s5), ALU.is_equal))

            def softmax_and_first_choice():
                dve.wait_ge(const_ready, 8)
                V.tensor_copy(count[:], count_i[:])
                dve.wait_ge(expd, 1)
                then(V.tensor_reduce(s1, score[:], AX.X, ALU.add))
                then(V.reciprocal(s2, s1))
                then(V.tensor_tensor(score[:], score[:], over_e(s2), ALU.mult))
                then(V.tensor_scalar(first[:], count[:, 0:E], -1.0, float(E), ALU.mult, ALU.add))
                V.tensor_scalar(count_r[:], count[:, 0:E], float(R), None, ALU.mult)

                best(0, score, s0)

            def second_choice():
                then(V.scalar_tensor_tensor(out=rest[:], in0=sel[0][:], scalar=-2.0, in1=score[:], op0=ALU.mult,
                                            op1=ALU.add))
                best(1, rest, s1)
                V.tensor_tensor(mask[:], sel[0][:], sel[1][:], ALU.add).then_inc(mask_ready, 1)
                then(V.tensor_tensor(s2, s0, s1, ALU.add))
                then(V.tensor_scalar(s3, s2, 1e-20, None, ALU.add))
                V.reciprocal(s4, s3).then_inc(sum_ready, 1)

            def bases_and_slots():
                dve.wait_ge(counts_ready, 1)
                then(V.tensor_reduce(tokens_e[:], total[:].rearrange("p t e -> p e t"), AX.X, ALU.add))
                then(V.tensor_tensor(square[:], tokens_e[:].unsqueeze(2).to_broadcast([P, E, E]),
                                     count_r[:].unsqueeze(1).to_broadcast([P, E, E]), ALU.is_gt))
                then(V.tensor_reduce(tiles_e[:], square[:], AX.X, ALU.add))
                then(V.tensor_tensor(square2[:], more[:], tiles_e[:].unsqueeze(1).to_broadcast([P, E, E]), ALU.mult))
                then(V.tensor_reduce(base_e[:], square2[:], AX.X, ALU.add))
                then(V.tensor_scalar(tiles_e[:], base_e[:], float(R), None, ALU.mult))

                dve.wait_ge(slot_step, SLOT_STEPS)
                then(V.tensor_tensor(slot[:], slot[:], tiles_e[:].unsqueeze(1).to_broadcast([P, T, E]), ALU.add))
                for k in range(TOP):
                    i = V.tensor_tensor(picked[k][:], sel[k][:], slot[:], ALU.mult)
                then(i)
                for k in range(TOP):
                    i = V.tensor_reduce(slot_f[k][:], picked[k][:], AX.X, ALU.add)
                then(i)
                for k in range(TOP):
                    i = V.tensor_copy(pos[:, k], slot_f[k][:])
                i.then_inc(pos_ready, 1)

            def owners():
                then(V.tensor_tensor(owner[:], base_e[0:1].unsqueeze(1).to_broadcast([1, ROUTED, E]),
                                     count[0:1].unsqueeze(2).to_broadcast([1, ROUTED, E]), ALU.is_gt))
                then(V.tensor_reduce(owner_f[:], owner[:], AX.X, ALU.add))
                V.tensor_copy(etab[0:1, 0:ROUTED], owner_f[:]).then_inc(etab_ready, 1)

            pieces = (softmax_and_first_choice, second_choice, bases_and_slots, owners)

            def weigh_shared(t):
                dve.wait_ge(d_done, t * 2 + 2)
                dve.wait_ge(s_res[t % 2], 16 * (t // 2 + 1))
                for j in range(QT):
                    i = V.scalar_tensor_tensor(out=ys[:, t % 2, j], in0=YB[j], scalar=tg[:, 1:2], in1=ys[:, t % 2, j],
                                               op0=ALU.mult, op1=ALU.add)
                i.then_inc(y_ready, 1)

            def weigh(t, p, routed):
                dve.wait_ge(d_done, t * 2 + 2)
                dve.wait_ge(meta_ready, t - (SHARED - 1))
                if isinstance(t, int) and t - 2 < SHARED:
                    dve.wait_ge(s_stored[p], 16 * (SHARED // 2))
                else:
                    dve.wait_ge(s_added, t * (16 * QT) - 16 * QT * (SHARED + 1))
                for j in range(QT):
                    i = V.tensor_scalar(ys[:, p, j], YB[j], meta[:, p, j, 1:2], None, ALU.mult)
                i.then_inc(y_ready, 1)

            def tile(t, p, routed, between=None):
                e0 = expert(dve, t) if routed(0) else None
                e2 = expert(dve, t + 2) if exists(t + 2) and routed(2) else None
                late = isinstance(t, int) and t == SHARED - 1
                begun = isinstance(t, int) and t == 0
                if exists(t + 1) and not late and not begun:
                    rows_low(t + 1, 1 - p)
                if e0 is not None:
                    split_low(cuts(t, True), 3, e0)
                if not isinstance(t, int) or t > 0:
                    hidden(t, 1)
                if late:
                    rows_low(t + 1, 1 - p)
                if not isinstance(t, int) or t > 0:
                    hidden_low(t, 1)
                if between:
                    between()
                if exists(t + 1) and not begun:
                    hidden(t + 1, 0)
                if e0 is not None:
                    weigh(t, p, routed)
                else:
                    weigh_shared(t)
                if exists(t + 1):
                    hidden_low(t + 1, 0)
                if e2 is not None:
                    split_low(cuts(t + 2, True), 0, e2)

            for t in range(SHARED):
                tile(t, t % 2, lambda d: t + d >= SHARED, pieces[2 * t] if 2 * t < len(pieces) else None)
                if 2 * t + 1 < len(pieces):
                    pieces[2 * t + 1]()
                if t == SHARED - 3:
                    dve.wait_ge(etab_ready, 1)
                    for e in range(E):
                        dve.wait_ge(s_raw[e], 48)
            tile(SHARED, 0, lambda d: d >= 0)
            tile(SHARED + 1, 1, lambda d: True)
            with dve.Fori(SHARED // 2 + 1, LAST_PAIR // 2) as u:
                for p in range(2):
                    tile(u * 2 + p, p, lambda d: True)
            for t in range(LAST_PAIR, TILES):
                tile(t, t % 2, lambda d: True)

        @block.tensor
        def _(pe):
            pe.wait_ge(ident_ready, 1)

            def transposes(n):
                pe.wait_ge(xn_ready, n + 1)
                if has(n - 2):
                    pe.wait_ge(p_lo, 2 * n - 2)
                for k in range(KT):
                    for j in range(QT):
                        i = nc.tensor.transpose(BC1[:, k * S + j * P:k * S + j * P + P], xn[:, j, k * P:(k + 1) * P],
                                                ident[:])
                i.then_inc(xT_done, 1)

            def context_transposes(g):
                pe.wait_ge(s_c, 16 * g + 16)
                pe.wait_ge(xT_lo, 2 * g + 1)
                for k in range(CT):
                    for n in range(2):
                        i = nc.tensor.transpose(BC1[0:CP, (k * 2 + n) * M:(k * 2 + n + 1) * M],
                                                crow[:, n, k * CP:(k + 1) * CP], ident[0:M, 0:M])
                i.then_inc(cT_done, 1)

            def product(dst, lhs, rhs, ks):
                for n, k in enumerate(ks):
                    for u, (a, c) in enumerate(PASSES):
                        i = nc.tensor.matmul(dst, lhs(a, k), rhs(c, k), start=(n == 0 and u == 0),
                                             stop=(n == len(ks) - 1 and u == 2))
                return i

            def projections(n, h):
                pe.wait_ge(xT_lo, n + 1)
                if has(n - 1):
                    pe.wait_ge(exp_ready, QT * n - 1)
                pe.wait_ge(wlo_ready, 1)
                for m in range(2):
                    mt = 2 * h + m
                    i = product((BA0, BA1)[h][:, m * S:(m + 1) * S], lambda a, k: wq_s[:, a, k, mt * P:(mt + 1) * P],
                                lambda a, k: xT[:, a, k], range(KT))
                i.then_inc(q_done, 1)

            def projected_keys(g):
                pe.wait_ge(cT_lo, g + 1)
                pe.wait_ge(wlo_ready, 2)
                if has(g - 1):
                    pe.wait_ge(exp_ready, 2 * QT * g)
                for m in range(MT):
                    i = product(psum[:, 2 + m // 2, (m % 2) * 2 * M:(m % 2 + 1) * 2 * M],
                                lambda a, k: wk_s[:, a, k, m * P:(m + 1) * P], lambda a, k: cT[:, a, k], range(CT))
                i.then_inc(k_done, 1)

            def scores(b, odd, g):
                pe.wait_ge(q_lo, 2 * b + 2)
                pe.wait_ge(k_lo, 2 * g + 2)
                for j in range(QT):
                    for m in range(PAIRS):
                        i = product(SCORES[j][:, m // 2, (m % 2) * 2 * M:(m % 2 + 1) * 2 * M],
                                    lambda a, k: qT[:, a, m, j * P:(j + 1) * P],
                                    lambda a, k: kz[:, a, m, odd].rearrange("p a k -> p (a k)"), (0,))
                    i.then_inc(s_done, 1)

            def values(b, odd):
                if has(b - 1):
                    pe.wait_ge(p_lo, 2 * b)
                pe.wait_ge(wlo_ready, 3)
                product(BE[0:M], lambda a, k: cT[:, a, k, odd * M:(odd + 1) * M], lambda a, k: wv_s[:, a, k], range(CT)) \
                    .then_inc(v_done, 1)

            def turn(b):
                pe.wait_ge(norm_ready, QT * b + QT)
                pe.wait_ge(v_lo, b + 1)
                for i in range(2):
                    if i == 1 and has(b - 1):
                        pe.wait_ge(y_added, b)
                    if i == 1 and has(b - 2):
                        pe.wait_ge(l_ready, b)
                    for hh in range(4):
                        h = 4 * i + hh
                        for j in range(QT):
                            t = nc.tensor.transpose(TURNED[i][0:M, hh // 2, (hh % 2) * S + j * P:(hh % 2) * S + j * P + P],
                                                    prob[:, j, h], ident[:])
                    t.then_inc(p_done, 1)

            def attend(b):
                for i, bank in enumerate((BD, BC0)):
                    pe.wait_ge(p_lo, 2 * b + i + 1)
                    for g in range(2):
                        h = 4 * i + 2 * g
                        t = product(bank[:, g * S:(g + 1) * S], lambda a, k: vz[:, a, k],
                                    lambda a, k: pT[:, a, k], (h, h + 1))
                    t.then_inc(o_done, 1)

            def project_out(b):
                pe.wait_ge(o_lo, 2 * b + 2)
                pe.wait_ge(wlo_ready, 4)
                if with_first_rows(b + 1):
                    pe.wait_ge(tx_lo, 1)
                for j in range(QT):
                    t = product(BC1[:, j * H:(j + 1) * H], lambda a, k: oT[:, a, k, j * P:(j + 1) * P],
                                lambda a, k: wo_s[:, a, k], range(MT))
                t.then_inc(y_done, 1)

            def transposes2(n):
                pe.wait_ge(xn2_ready, n + 1)
                if has(n + 1):
                    pe.wait_ge(o_lo, 2 * n + 4)
                for k in range(KT):
                    for j in range(QT):
                        i = nc.tensor.transpose(BC0[:, k * S + j * P:k * S + j * P + P], xn2[:, j, k * P:(k + 1) * P],
                                                ident[:])
                i.then_inc(x2_done, 1)

            def logits(n):
                pe.wait_ge(x2_lo, n + 1)
                pe.wait_ge(gw_lo, 1)
                for j in range(QT):
                    i = product(BC0[:, j * E:(j + 1) * E], lambda a, k: x2T[:, a, k, j * P:(j + 1) * P],
                                lambda a, k: gw_s[:, a, k], range(KT))
                i.then_inc(l_done, 1)

            def rows_in(t, p):
                pe.wait_ge(x_loaded[p], (t // 2 + 1) * 16 if isinstance(t, int) else t * 8 + (16 - 8 * p))
                if not isinstance(t, int) or t > 0:
                    pe.wait_ge(tx_lo, t)
                for k in range(KT):
                    for j in range(QT):
                        i = nc.tensor.transpose(rows_bank(t)[:, k * R + j * P:k * R + j * P + P], xin[:, p, j, k * P:(k + 1) * P],
                                                ident[:])
                i.then_inc(tx_done, 1)

            def gate_up(t, p, h, routed):
                pe.wait_ge(w_lo[h], cuts(t, routed))
                pe.wait_ge(tx_lo, t + 1)
                if not isinstance(t, int) or t >= 1:
                    pe.wait_ge(h_ready, t * 2 + h - 1)
                for c, bank in ((0, GATE[h]), (1, UP[h])):
                    for m in range(KD // 2):
                        i = product(bank[:, m * R:(m + 1) * R],
                                    lambda a, k: wgu[h][:, a, c * KT + k, m * P:(m + 1) * P],
                                    lambda a, k: tx[p][:, a, k], range(KT))
                i.then_inc(gu_done, 1)

            def step(b, odd, g):
                if has(b - 1):
                    turn(b - 1)
                if has(b):
                    scores(b, odd, g)
                if has(b + 1):
                    transposes(b + 1)
                if is_last(b):
                    gate_up(0, 0, 0, False)
                if has(b - 1):
                    attend(b - 1)
                if has(b) and has(b - 1):
                    values(b, odd)
                if with_first_rows(b):
                    rows_in(0, 0)
                if odd and more_context(g):
                    context_transposes(g + 1)
                if has(b + 1):
                    projections(b + 1, 0)
                if has(b - 2):
                    transposes2(b - 2)
                if has(b + 1):
                    projections(b + 1, 1)
                if odd and more_context(g):
                    projected_keys(g + 1)
                if has(b - 1):
                    project_out(b - 1)
                if is_last(b):
                    rows_in(1, 1)
                    gate_up(0, 0, 1, False)
                if has(b - 2):
                    logits(b - 2)

            transposes(0)
            context_transposes(0)
            projections(0, 0)
            projections(0, 1)
            projected_keys(0)
            values(0, 0)
            over_batches(pe, step)
            pe.wait_ge(l_ready, B)
            transposes2(B - 1)
            gate_up(1, 1, 0, False)
            logits(B - 1)

            def count_prefixes():
                pe.wait_ge(mask_ready, 1)
                m = mask[:].rearrange("p t e -> p (t e)")
                nc.tensor.matmul(BE[:, 0:T * E], before[:], m, start=True, stop=True)
                nc.tensor.matmul(BE[:, T * E:2 * T * E], ones[:], m, start=True, stop=True).then_inc(prefix_done, 1)

            def down(t, h, routed):
                pe.wait_ge(w_lo[2 + h], cuts(t, routed))
                pe.wait_ge(h_lo, t * 2 + h + 1)
                if isinstance(t, int) and t == 0 and h == 0:
                    pe.wait_ge(l_ready, B + 1)
                elif h == 0:
                    pe.wait_ge(y_ready, t)
                for j in range(QT):
                    for m in range(KD // 2):
                        for u, (a, c) in enumerate(PASSES):
                            i = nc.tensor.matmul(YB[j], hs[h][:, a, m, j * P:(j + 1) * P], wdn[h][:, c, m],
                                                 start=(h == 0 and m == 0 and u == 0),
                                                 stop=(h == 1 and m == KD // 2 - 1 and u == 2))
                i.then_inc(d_done, 1)

            def tile(t, p, routed):
                late = isinstance(t, int) and t == SHARED - 1
                begun = isinstance(t, int) and t == 0
                if exists(t + 1) and not late and not begun:
                    rows_in(t + 1, 1 - p)
                if not begun:
                    gate_up(t, p, 1, routed(0))
                if late:
                    rows_in(t + 1, 1 - p)
                down(t, 0, routed(0))
                if isinstance(t, int) and t == 1:
                    count_prefixes()
                if exists(t + 1) and not begun:
                    gate_up(t + 1, 1 - p, 0, routed(1))
                down(t, 1, routed(0))

            over_tiles(pe, tile)


_INS = ['x', 'ctx_768', 'g_xattn', 'g_ffn', 'L0_xattn_Wq', 'L0_xattn_Wk', 'L0_xattn_Wv', 'L0_xattn_Wout',
        'L0_xattn_bout', 'L0_ffn_gate_w', 'L0_ffn_w_gate', 'L0_ffn_w_up', 'L0_ffn_w_down', 'L0_ffn_ws_gate',
        'L0_ffn_ws_up', 'L0_ffn_ws_down']
_OUT = (8, 256, 256)
_SPARE = 256


def kernel(**inputs):
    import numpy as _np
    import concourse.bacc as _bacc
    from concourse import mybir as _mybir
    from concourse.bass_utils import run_bass_kernel_spmd as _run

    nc = _bacc.Bacc("TRN2", target_bir_lowering=False, num_devices=1)
    arrays, args = {}, []
    for name in _INS:
        a = _np.ascontiguousarray(inputs[name])
        arrays[f"in_{name}_dram"] = a
        args.append(nc.dram_tensor(f"in_{name}_dram", a.shape, _mybir.dt.from_np(a.dtype), kind="ExternalInput").ap())
    out = nc.dram_tensor("out_dram", (_OUT[0] * _OUT[1] + _SPARE, _OUT[2]), _mybir.dt.float32, kind="ExternalOutput").ap()
    build(nc, *args, out)
    r = _run(nc, [arrays], core_ids=[0])
    return r.results[0]["out_dram"][:_OUT[0] * _OUT[1]].reshape(_OUT)
```
